# Optimizing a Trainium2 kernel written in Bass

```python
import numpy as np
import jax
import jax.numpy as jnp

def _softmax(x, axis=-1):
    return jax.nn.softmax(x, axis=axis)

def _gelu(x):
    return jax.nn.gelu(x, approximate=True)

def _silu(x):
    return jax.nn.silu(x)

def _sigmoid(x):
    return jax.nn.sigmoid(x)

def _layernorm(x, axis=-1, eps=1e-05):
    m = jnp.mean(x, axis=axis, keepdims=True)
    v = jnp.var(x, axis=axis, keepdims=True)
    return (x - m) / jnp.sqrt(v + eps)

def _scatter_add(tgt, idx, src, axis=0):
    return tgt.at[idx].add(src)

def _segment_sum(src, seg, n):
    return jax.ops.segment_sum(src, seg, n)
kernel_name = 'mk_recurrent_d1_jaxref_r4_7fabcd'

def setup_inputs(seed: int=0):
    np.random.seed(seed)
    _w = jnp.asarray

    def _L0_attn_setup():
        import jax, jax.numpy as jnp
        import numpy as np
        B, S, D = (4, 512, 256)
        SCALE = 1.0 / np.sqrt(D)
        key = jax.random.key(seed)
        k1, k2, k3 = jax.random.split(key, 3)
        x = jax.random.normal(k1, (B, S, D), dtype=jnp.float32)
        bound = 1.0 / np.sqrt(D)
        W_qk = jax.random.uniform(k2, (D, D), minval=-bound, maxval=bound, dtype=jnp.float32)
        W_v = jax.random.uniform(k3, (D, D), minval=-bound, maxval=bound, dtype=jnp.float32)
        alibi_slope = jnp.full((1,), 0.5, dtype=jnp.float32)
        return {'x': x, 'W_qk': W_qk, 'W_v': W_v, 'alibi_slope': alibi_slope}
    _L0_attn_in = _L0_attn_setup()

    def _L0_ffn_setup():
        import math
        import jax, jax.numpy as jnp
        import numpy as np
        B, S, D, F, E = (8, 512, 256, 1024, 8)
        CAPACITY_FACTOR = 1.0
        key = jax.random.key(seed)
        k1, k2, k3, k4 = jax.random.split(key, 4)
        x = jax.random.normal(k1, (B, S, D), dtype=jnp.float32)
        Wr = jax.random.normal(k2, (D, E), dtype=jnp.float32) * (1.0 / math.sqrt(D))
        W1 = jax.random.normal(k3, (E, D, F), dtype=jnp.float32) * (1.0 / math.sqrt(D))
        W2 = jax.random.normal(k4, (E, F, D), dtype=jnp.float32) * (1.0 / math.sqrt(F))
        return {'x': x, 'Wr': Wr, 'W1': W1, 'W2': W2}
    _L0_ffn_in = _L0_ffn_setup()
    _d = {'L0_attn_x': _L0_attn_in['x'], 'L0_attn_W_qk': _L0_attn_in['W_qk'], 'L0_attn_W_v': _L0_attn_in['W_v'], 'L0_attn_alibi_slope': _L0_attn_in['alibi_slope'], 'L0_ffn_Wr': _L0_ffn_in['Wr'], 'L0_ffn_W1': _L0_ffn_in['W1'], 'L0_ffn_W2': _L0_ffn_in['W2']}
    _x0 = _d['L0_attn_x']
    _d['L0_attn_x'] = jax.random.normal(jax.random.fold_in(jax.random.key(seed), 1), (2, 2048, 256), dtype=_x0.dtype)
    del _x0
    return _d

def reference(L0_attn_x, L0_attn_W_qk, L0_attn_W_v, L0_attn_alibi_slope, L0_ffn_Wr, L0_ffn_W1, L0_ffn_W2):

    def _L0_attn_ref(x, W_qk, W_v, alibi_slope):
        import jax, jax.numpy as jnp
        import numpy as np
        B, S, D = (4, 512, 256)
        SCALE = 1.0 / np.sqrt(D)
        seq_len = x.shape[1]
        scores = jnp.einsum('bqe,bke->bqk', x @ W_qk, x) * SCALE
        kpos = jnp.arange(seq_len, dtype=x.dtype)[None, :]
        qpos = jnp.arange(seq_len, dtype=x.dtype)[:, None]
        scores = scores + (kpos - qpos) * alibi_slope[0]
        causal = qpos >= kpos
        scores = jnp.where(causal, scores, -jnp.inf)
        attn = jax.nn.softmax(scores, axis=-1)
        v = x @ W_v.T
        return jnp.einsum('bqk,bkd->bqd', attn, v)

    def _L0_ffn_ref(x, Wr, W1, W2):
        import math
        import jax, jax.numpy as jnp
        import numpy as np
        B, S, D, F, E = (8, 512, 256, 1024, 8)
        CAPACITY_FACTOR = 1.0
        b, s, d = x.shape
        t = b * s
        cap = max(math.ceil(t * CAPACITY_FACTOR / E), 1)
        xf = x.reshape(t, d)
        probs = jax.nn.softmax(xf.astype(jnp.float32) @ Wr, axis=-1)
        eidx = jnp.argmax(probs, axis=-1)
        p_tok = jnp.take_along_axis(probs, eidx[:, None], axis=1)[:, 0]
        onehot = jax.nn.one_hot(eidx, E, dtype=jnp.int32)
        rank_all = jnp.cumsum(onehot, axis=0) - onehot
        rank = jnp.take_along_axis(rank_all, eidx[:, None], axis=1)[:, 0]
        keep = rank < cap
        slot = jnp.where(keep, rank, cap)
        dispatch = jnp.zeros((E, cap + 1), dtype=jnp.int32).at[eidx, slot].set(jnp.arange(t, dtype=jnp.int32))
        valid = jnp.zeros((E, cap + 1), dtype=bool).at[eidx, slot].set(keep)
        dispatch = dispatch[:, :cap]
        valid = valid[:, :cap]
        xe = xf[dispatch]
        h = jnp.maximum(jnp.einsum('ecd,edf->ecf', xe, W1), 0.0)
        ye = jnp.einsum('ecf,efd->ecd', h, W2)
        pe = p_tok[dispatch]
        ye = ye * (pe * valid.astype(ye.dtype))[:, :, None]
        y = jnp.zeros((t, d), dtype=x.dtype).at[dispatch.reshape(-1)].add(ye.reshape(E * cap, d).astype(x.dtype))
        return y.reshape(b, s, d)
    x = L0_attn_x
    xn = _layernorm(x, axis=-1)
    s = _L0_attn_ref(xn, L0_attn_W_qk, L0_attn_W_v, L0_attn_alibi_slope)
    g = _silu(_L0_ffn_ref(xn, L0_ffn_Wr, L0_ffn_W1, L0_ffn_W2))
    x = x + s * g
    return x

_drawn_inputs = setup_inputs


def setup_inputs(seed=0):
    import zlib

    import numpy as np

    out = dict(_drawn_inputs(seed))
    spreads = {}
    factors = {'L0_attn_W_qk': 3.262}
    for name, (base, spread) in spreads.items():
        noise = np.random.default_rng([zlib.crc32(name.encode()), seed]).standard_normal(out[name].shape)
        drawn = base * np.exp(spread * noise) if base else spread * noise
        out[name] = jnp.asarray(drawn.astype(out[name].dtype))
    for name, factor in factors.items():
        out[name] = (out[name] * factor).astype(out[name].dtype)
    return out
```

```python
from contextlib import ExitStack

import concourse.bass as bass
from concourse import mybir

P = 128
B, S, D = 2, 2048, 256
E, F = 8, 1024
T = B * S
CAP = T // E
KD = D // P
NT = S // P
GT = 4
GTOK = GT * P
NG = NT // GT
NF = F // P
SJ = CAP // P
ROW = D + 8
PCOL, TCOL = D, D + 1
NOWHERE = float(1 << 20)
PIECE = 512
WCOLS = KD * F
PIECES = WCOLS // PIECE

X_UP = 2.0 ** 10
ACC_DOWN = 2.0 ** -18
W_TOP = 14
UNDO = 2.0 ** 8
SM_SCALE = 2.0 ** -4
LN2_UP = 14 * 0.6931471805599453
EPS = 1e-5

NCHUNK = sum(i // GT + 1 for i in range(NT))
UNITS = 2 + GT + 2 + 1
NUNIT = NG * UNITS
LOOP_STEPS = NG * 15 + NT * 3 + 4
PAIR_STEPS = 2 * 4

F32 = mybir.dt.float32
F16 = mybir.dt.float16
I32 = mybir.dt.int32
U32 = mybir.dt.uint32
ALU = mybir.AluOpType
ACT = mybir.ActivationFunctionType
AX = mybir.AxisListType
RMAX = bass.bass_isa.ReduceOp.absmax


def chunks(i):
    return i // GT + 1


def chunk_no(i, c):
    return sum(chunks(k) for k in range(i)) + c


def chunk_blocks(i, c):
    return GT if c < chunks(i) - 1 else i % GT + 1


def layer_kernel(nc, x, w_qk, w_v, slope, w_r, w_e, out, slots, rows):
    with ExitStack() as ctx:
        def sb(name, shape, dt=F32):
            return ctx.enter_context(nc.sbuf_tensor(name, shape, dt))

        def sem(name):
            return ctx.enter_context(nc.semaphore(name))

        ident = sb("ident", [P, P])
        before = sb("before", [P, P], F16)
        ones = sb("ones", [P, P], F16)
        ranks = sb("ranks", [P, GT, E])
        bias = sb("bias", [P, S])
        slope_c = sb("slope_c", [P, 1])
        wsmall = sb("wsmall", [P, 3, KD, D])
        wqk_h = sb("wqk_h", [P, KD, D], F16)
        wqk_l = sb("wqk_l", [P, KD, D], F16)
        wvr_h = sb("wvr_h", [P, KD, D + E], F16)
        wvr_l = sb("wvr_l", [P, KD, D + E], F16)
        small_max = sb("small_max", [P, 3])
        small_top = sb("small_top", [P, 3])
        small_exp = sb("small_exp", [P, 3])
        small_up = sb("small_up", [P, 3])
        small_dn = sb("small_dn", [P, 3])
        score_mul = sb("score_mul", [P, 1])
        bias_mul = sb("bias_mul", [P, 1])
        value_mul = sb("value_mul", [P, 1])
        logit_mul = sb("logit_mul", [P, 1])
        empty = sb("empty", [P, ROW])

        xg = [sb(f"xg{k}", [P, GT, 2 * D]) for k in range(2)]
        xnr = [sb(f"xnr{k}", [P, GT, ROW]) for k in range(2)]
        stats = sb("stats", [P, GT, 6])
        mv = sb("mv", [P, GT, 2])
        var = sb("var", [P, GT])
        std = sb("std", [P, GT])
        rec = sb("rec", [P, GT])
        sq = sb("sq", [P, GT])
        sqv = sb("sqv", [P, GT])
        rstd = sb("rstd", [P, GT])
        xT_h = sb("xT_h", [P, KD, S], F16)
        xT_l = sb("xT_l", [P, KD, S], F16)
        v_h = sb("v_h", [P, NT, D], F16)
        v_l = sb("v_l", [P, NT, D], F16)
        qT_h = [sb(f"qT_h{k}", [P, KD, GTOK], F16) for k in range(2)]
        qT_l = [sb(f"qT_l{k}", [P, KD, GTOK], F16) for k in range(2)]
        logits = sb("logits", [P, GT, E])
        lmax = sb("lmax", [P, GT])
        below = sb("below", [P, GT, E])
        lexp = sb("lexp", [P, GT, E])
        lsum = sb("lsum", [P, GT])
        key = sb("key", [P, GT, E])
        kmax = sb("kmax", [P, GT])
        chosen = sb("chosen", [P, GT, E], F16)
        place = sb("place", [P, GT, E])
        placed = sb("placed", [P, GT, E])
        slot = sb("slot", [P, GT])
        limit = sb("limit", [P, GT])
        keep = sb("keep", [P, GT])
        kept = sb("kept", [P, GT])
        slot_idx = [sb(f"slot_idx{k}", [P, GT], U32) for k in range(2)]
        taken = sb("taken", [P, E])
        token = sb("token", [P, GT])

        sc = sb("sc", [P, 2, S])
        cmax = sb("cmax", [P, 2, NG])
        rmax = sb("rmax", [P, 2])
        nbias = sb("nbias", [P, 2])
        psums = sb("psums", [P, 2, NG])
        rsum = sb("rsum", [P, 2])
        rinv = sb("rinv", [P, 2])
        pT_h = sb("pT_h", [P, 2, S], F16)
        pT_l = sb("pT_l", [P, 2, S], F16)

        raw = sb("raw", [P, 2, WCOLS])
        wraw = [raw, sc]
        w_h = [sb(f"w_h{k}", [P, 2, WCOLS], F16) for k in range(2)]
        w_l = [sb(f"w_l{k}", [P, 2, WCOLS], F16) for k in range(2)]
        wmax = sb("wmax", [P, 2])
        wtop = sb("wtop", [P, 2])
        wexp = sb("wexp", [P, 2])
        wup = [sb(f"wup{k}", [P, 2]) for k in range(2)]
        wdn = sb("wdn", [P, 2])
        ymul = [sb(f"ymul{k}", [P, 1]) for k in range(2)]
        xe = sb("xe", [P, SJ, ROW])
        xeT_h = [sb(f"xeT_h{k}", [P, KD, CAP], F16) for k in range(2)]
        xeT_l = [sb(f"xeT_l{k}", [P, KD, CAP], F16) for k in range(2)]
        pk = [sb(f"pk{k}", [P, SJ]) for k in range(2)]
        get_idx = [sb(f"get_idx{k}", [P, SJ], U32) for k in range(2)]
        put_idx = [sb(f"put_idx{k}", [P, SJ], U32) for k in range(2)]
        hid = sb("hid", [P, 2, CAP])
        hid_h = sb("hid_h", [P, 2, CAP], F16)
        hid_l = sb("hid_l", [P, 2, CAP], F16)
        gate = sb("gate", [P, SJ, D])
        gated = sb("gated", [P, SJ, D])
        back = [sb(f"back{j}", [P, 2 * D]) for j in range(SJ)]
        done = [sb(f"done{j}", [P, D]) for j in range(SJ)]

        bank = [ctx.enter_context(nc.psum_tensor(f"bank{k}", [P, 512], F32)) for k in range(8)]
        sc_ps, tr_ps, pv_ps, aux = bank[0:2], bank[2:4], bank[4:6], bank[6:8]
        y_ps = bank[2:6]

        x_in = [sem(f"x_in{k}") for k in range(2)]
        small_in = sem("small_in")
        slots_empty = sem("slots_empty")
        out_first = [sem(f"out_first{k}") for k in range(2)]
        rows_out = [sem(f"rows_out{k}") for k in range(2)]
        slots_out = [sem(f"slots_out{k}") for k in range(2)]
        w_in = sem("w_in")
        w_in_odd = sem("w_in_odd")
        xe_in = sem("xe_in")
        back_in = [sem(f"back_in{j}") for j in range(SJ)]
        out_put = [sem(f"out_put{j}") for j in range(SJ)]
        consts_made = sem("consts_made")
        small_maxed = sem("small_maxed")
        small_topped = sem("small_topped")
        wv_turned = sem("wv_turned")
        bias_made = sem("bias_made")
        setup_step = sem("setup_step")
        ready = sem("ready")
        bias_raw = sem("bias_raw")
        pool_step = sem("pool_step")
        dve_step = sem("dve_step")
        var_made = sem("var_made")
        std_made = sem("std_made")
        xn_made = sem("xn_made")
        aux_full = sem("aux_full")
        aux_read = sem("aux_read")
        hi_made = sem("hi_made")
        below_made = sem("below_made")
        lexp_made = sem("lexp_made")
        chosen_made = sem("chosen_made")
        token_set = sem("token_set")
        prob_set = sem("prob_set")
        slot_made = sem("slot_made")
        score_full = sem("score_full")
        score_read = sem("score_read")
        nbias_made = sem("nbias_made")
        exp_made = sem("exp_made")
        turned = sem("turned")
        pT_hi = sem("pT_hi")
        pT_lo = sem("pT_lo")
        pv_full = sem("pv_full")
        s_made = sem("s_made")
        w_maxed = sem("w_maxed")
        w_topped = sem("w_topped")
        w_scaled = sem("w_scaled")
        w_hi = sem("w_hi")
        w_lo = sem("w_lo")
        xe_turned = sem("xe_turned")
        xe_hi = sem("xe_hi")
        xe_lo = sem("xe_lo")
        idx_made = sem("idx_made")
        h_full = sem("h_full")
        h_read = sem("h_read")
        h_hi = sem("h_hi")
        h_lo = sem("h_lo")
        y_full = sem("y_full")
        gate_made = sem("gate_made")
        gate_used = sem("gate_used")
        gated_made = sem("gated_made")
        done_made = sem("done_made")
        passed = sem("passed")

        x_g = x.rearrange("(g j p) d -> g p j d", p=P, j=GT)
        out_g = out.rearrange("(g j p) d -> g p j d", p=P, j=GT)
        rows_g = rows.rearrange("(g j p) d -> g p j d", p=P, j=GT)
        slots_e = slots.rearrange("(e j p) d -> e p j d", p=P, j=SJ)
        w_k = w_e.rearrange("e k p n -> e p k n")

        block = ctx.enter_context(nc.Block())

        def steps(i):
            nxt = chunks(i + 1) if i + 1 < NT else 0
            for c in range(max(nxt, chunks(i) + 1)):
                yield (c if c < nxt else None, c if c < chunks(i) else None,
                       c - 1 if 0 <= c - 1 < chunks(i) else None)

        def units_after(i):
            g, j = divmod(i, GT)
            if g + 1 == NG:
                return []
            return {0: [], 1: [0, 1, 2, 3], 2: [4, 5, 6, 7], 3: [8]}[j]

        def norm_after(i):
            return i % GT == 0 and i // GT + 1 < NG

        def apart(eng):
            eng.sem_inc(passed, 1)

        @block.sync
        def _(sp):
            sp.dma_start(wsmall[:, 0], w_qk.rearrange("(k p) n -> p k n", p=P)).then_inc(small_in, 16)
            sp.dma_start(wsmall[:, 1], w_v.rearrange("(k p) n -> p k n", p=P)).then_inc(small_in, 16)
            sp.dma_start(wsmall[:, 2, :, 0:E], w_r.rearrange("(k p) n -> p k n", p=P)).then_inc(small_in, 16)
            sp.dma_start(slope_c[:, :], slope.rearrange("(o n) -> o n", o=1).partition_broadcast(P)
                         ).then_inc(small_in, 16)
            sp.wait_ge(consts_made, 1)
            for k in range(T // P):
                sp.dma_start(slots[k * P:(k + 1) * P, :], empty[:, :]).then_inc(slots_empty, 16)
            with sp.Fori(0, B) as b:
                for g in range(NG):
                    k = g % 2
                    if g == 0:
                        sp.dma_start(xg[0][:, :, 0:D], x_g[bass.ds(b * NG, 1)]).then_inc(x_in[0], 16)
                        sp.dma_start(raw[:, bass.ds(b, 1), :], w_k[0][:, bass.ds(b, 1), :]).then_inc(w_in, 16)
                    if g + 1 < NG:
                        if g:
                            n = (g + 1) // 2 * 16
                            sp.wait_ge(rows_out[1 - k], b * 32 + n)
                            sp.wait_ge(out_first[1 - k], b * 32 + n)
                        sp.dma_start(xg[1 - k][:, :, 0:D], x_g[bass.ds(b * NG + g + 1, 1)]
                                     ).then_inc(x_in[1 - k], 16)
                    sp.wait_ge(x_in[k], b * 32 + g // 2 * 16 + 16)
                    sp.dma_start(out_g[bass.ds(b * NG + g, 1)], xg[k][:, :, 0:D]).then_inc(out_first[k], 16)
                    sp.wait_ge(s_made, b * NT + (g + 1) * GT + 1)
                    sp.dma_start(rows_g[bass.ds(b * NG + g, 1)], xg[k][:, :, :]).then_inc(rows_out[k], 16)
                for k in range(2):
                    sp.wait_ge(rows_out[k], b * 32 + 32)
                    sp.wait_ge(out_first[k], b * 32 + 32)
                apart(sp)

            for k in range(2):
                sp.wait_ge(slots_out[k], B * NG // 2 * GT * 16)
            sp.dma_start(xe[:, :, :], slots_e[0]).then_inc(xe_in, 16)
            sp.dma_start(wraw[1][:, :, :], w_k[1]).then_inc(w_in_odd, 16)

            def next_rows(e):
                sp.wait_ge(xe_turned, (e + 1) * KD)
                sp.wait_ge(idx_made, e + 1)
                sp.dma_start(xe[:, :, :], slots_e[bass.ds(e + 1, 1)]).then_inc(xe_in, 16)

            def next_weights(e, k):
                sp.wait_ge(w_lo, (e + 1) * 2 * PIECES)
                sp.dma_start(wraw[k][:, :, :], w_k[bass.ds(e + 2, 1)]).then_inc([w_in, w_in_odd][k], 16)

            with sp.Fori(0, E // 2 - 1) as i:
                for k in range(2):
                    next_rows(i * 2 + k)
                    next_weights(i * 2 + k, k)
            next_rows(E - 2)

        @block.gpsimd
        def _(pool):
            nc.gpsimd.memset(empty[:, :], 0.0).then_inc(pool_step, 1)
            pool.wait_ge(pool_step, 1)
            nc.gpsimd.memset(empty[:, TCOL:TCOL + 1], NOWHERE).then_inc(consts_made, 1)
            nc.gpsimd.memset(ident[:, :], 0.0).then_inc(pool_step, 1)
            nc.gpsimd.memset(ones[:, :], 1.0).then_inc(pool_step, 1)
            pool.wait_ge(pool_step, 3)
            nc.gpsimd.affine_select(out=ident[:, :], in_=ident[:, :], compare_op=ALU.not_equal, fill=1.0, base=0,
                                    pattern=[[-1, P]], channel_multiplier=1).then_inc(consts_made, 1)
            nc.gpsimd.affine_select(out=before[:, :], in_=ones[:, :], compare_op=ALU.is_gt, fill=0.0, base=0,
                                    pattern=[[1, P]], channel_multiplier=-1).then_inc(consts_made, 1)
            nc.gpsimd.iota(ranks[:, :, :], pattern=[[0, GT], [-1, E]], base=E, channel_multiplier=0,
                           allow_small_or_imprecise_dtypes=True).then_inc(consts_made, 1)
            nc.gpsimd.iota(taken[:, :], pattern=[[CAP, E]], base=0, channel_multiplier=0,
                           allow_small_or_imprecise_dtypes=True).then_inc(consts_made, 1)
            nc.gpsimd.iota(token[:, :], pattern=[[P, GT]], base=0, channel_multiplier=1,
                           allow_small_or_imprecise_dtypes=True).then_inc(consts_made, 1)
            nc.gpsimd.iota(bias[:, :], pattern=[[1, S]], base=P - S, channel_multiplier=-1,
                           allow_small_or_imprecise_dtypes=True).then_inc(bias_raw, 1)
            for k in range(2):
                nc.gpsimd.memset(xnr[k][:, :, :], 0.0).then_inc(consts_made, 1)
            pool.wait_ge(small_maxed, 1)
            nc.gpsimd.partition_all_reduce(small_top[:, :], small_max[:, :], P, RMAX).then_inc(small_topped, 1)
            pool.wait_ge(bias_made, 1)
            nc.gpsimd.affine_select(out=bias[:, S - P:S], in_=bias[:, S - P:S], compare_op=ALU.is_ge, fill=-3e38,
                                    base=0, pattern=[[-1, P]], channel_multiplier=1).then_inc(ready, 1)
            pool.wait_ge(slots_empty, 16 * (T // P))
            with pool.Fori(0, B) as b:
                for g in range(NG):
                    k = g % 2
                    pool.wait_ge(xn_made, b * NG + g + 1)
                    apart(pool)
                    nc.gpsimd.tensor_copy(xnr[k][:, :, TCOL], token[:, :]).then_inc(token_set, 1)
                    pool.wait_ge(token_set, b * NG + g + 1)
                    apart(pool)
                    nc.gpsimd.tensor_scalar(token[:, :], token[:, :], float(GTOK), None, ALU.add
                                            ).then_inc(pool_step, 1)
                    pool.wait_ge(pool_step, b * NG + g + 4)
                    pool.wait_ge(prob_set, b * NG + g + 1)
                    pool.wait_ge(slot_made, b * NG + g + 1)
                    apart(pool)
                    for j in range(GT):
                        nc.gpsimd.indirect_dma_start(
                            slots[:, :], bass.IndirectOffsetOnAxis(ap=slot_idx[k][:, j:j + 1], axis=0),
                            xnr[k][:, j, :], None, bounds_check=T - 1, oob_is_err=False).then_inc(slots_out[k], 16)
                    if g == 2:
                        pool.wait_ge(w_maxed, b + 1)
                        apart(pool)
                        nc.gpsimd.partition_all_reduce(wtop[:, :], wmax[:, :], P, RMAX).then_inc(w_topped, 1)

            def fetch(e, k, j):
                nc.gpsimd.indirect_dma_start(
                    back[j][:, :], None, rows[:, :],
                    bass.IndirectOffsetOnAxis(ap=get_idx[k][:, j:j + 1], axis=0)).then_inc(back_in[j], 16)

            for k in range(2):
                pool.wait_ge(rows_out[k], B * NG // 2 * 16)
                pool.wait_ge(out_first[k], B * NG // 2 * 16)
            pool.wait_ge(idx_made, 1)
            for j in range(SJ):
                fetch(0, 0, j)

            def expert(e, k, more):
                if more:
                    pool.wait_ge(w_maxed, e + B + 1)
                    apart(pool)
                    nc.gpsimd.partition_all_reduce(wtop[:, :], wmax[:, :], P, RMAX).then_inc(w_topped, 1)
                for j in range(SJ):
                    pool.wait_ge(gate_made, e * SJ + j + 1 + SJ)
                    pool.wait_ge(back_in[j], e * 16 + 16)
                    nc.gpsimd.tensor_tensor(gated[:, j, :], gate[:, j, :], back[j][:, D:2 * D], ALU.mult
                                            ).then_inc(gate_used, 1)
                for j in range(SJ):
                    pool.wait_ge(gate_used, e * SJ + j + 1 + SJ)
                    nc.gpsimd.tensor_tensor(done[j][:, :], gated[:, j, :], back[j][:, 0:D], ALU.add
                                            ).then_inc(done_made, 1)
                for j in range(SJ):
                    pool.wait_ge(done_made, e * SJ + j + 1)
                    apart(pool)
                    nc.gpsimd.indirect_dma_start(
                        out[:, :], bass.IndirectOffsetOnAxis(ap=put_idx[k][:, j:j + 1], axis=0),
                        done[j][:, :], None, bounds_check=T - 1, oob_is_err=False).then_inc(out_put[j], 16)
                if more:
                    for j in range(SJ):
                        pool.wait_ge(out_put[j], e * 16 + 16)
                    pool.wait_ge(idx_made, e + 2)
                    apart(pool)
                    for j in range(SJ):
                        fetch(e + 1, 1 - k, j)

            pool.sem_inc(gate_used, SJ)
            pool.sem_inc(gate_made, SJ)
            with pool.Fori(0, E // 2 - 1) as i:
                for k in range(2):
                    expert(i * 2 + k, k, True)
            expert(E - 2, 0, True)
            expert(E - 1, 1, False)
            for j in range(SJ):
                pool.wait_ge(out_put[j], 16 * E)

        @block.vector
        def _(dve):
            count = [0]

            def step(ins, at, alone=False):
                count[0] += 1
                ins.then_inc(dve_step, 1)
                dve.wait_ge(dve_step, at + count[0])
                if alone:
                    apart(dve)

            dve.wait_ge(small_in, 64)
            v = nc.vector
            v.memset(wmax[:, :], 0.0)
            v.tensor_reduce(small_max[:, 0:1], wsmall[:, 0], AX.XY, ALU.max, apply_absolute_value=True)
            v.tensor_reduce(small_max[:, 1:2], wsmall[:, 1], AX.XY, ALU.max, apply_absolute_value=True)
            v.tensor_reduce(small_max[:, 2:3], wsmall[:, 2, :, 0:E], AX.XY, ALU.max, apply_absolute_value=True
                            ).then_inc(small_maxed, 1)

            def scales(top, exp, up, dn, at):
                step(v.tensor_scalar(exp, top, 2.0 ** -100, None, ALU.max), at)
                step(v.tensor_scalar(exp.bitcast(I32), exp.bitcast(I32), 0x7F800000, None, ALU.bitwise_and), at)
                step(v.tensor_scalar(up.bitcast(I32), exp.bitcast(I32), float((2 * 127 + W_TOP) << 23), -1.0,
                                     ALU.subtract, ALU.mult), at)
                step(v.tensor_scalar(dn.bitcast(I32), exp.bitcast(I32), float(W_TOP << 23), None, ALU.subtract), at)

            dve.wait_ge(small_topped, 1)
            scales(small_top[:, :], small_exp[:, :], small_up[:, :], small_dn[:, :], 0)
            v.tensor_scalar(score_mul[:, :], small_dn[:, 0:1], SM_SCALE * UNDO / X_UP, None, ALU.mult)
            v.tensor_scalar(bias_mul[:, :], small_up[:, 0:1], X_UP / (SM_SCALE * UNDO), None, ALU.mult)
            v.tensor_scalar(value_mul[:, :], small_dn[:, 1:2], UNDO, None, ALU.mult)
            v.tensor_scalar(logit_mul[:, :], small_dn[:, 2:3], 1.0 / X_UP, None, ALU.mult)
            step(v.tensor_scalar(wqk_h[:, :, :], wsmall[:, 0], small_up[:, 0:1], None, ALU.mult), 0)
            v.scalar_tensor_tensor(wqk_l[:, :, :], wsmall[:, 0], small_up[:, 0:1], wqk_h[:, :, :],
                                   ALU.mult, ALU.subtract)
            step(v.tensor_scalar(wvr_h[:, :, D:D + E], wsmall[:, 2, :, 0:E], small_up[:, 2:3], None, ALU.mult), 0)
            v.scalar_tensor_tensor(wvr_l[:, :, D:D + E], wsmall[:, 2, :, 0:E], small_up[:, 2:3],
                                   wvr_h[:, :, D:D + E], ALU.mult, ALU.subtract)
            dve.wait_ge(bias_raw, 1)
            v.tensor_scalar(bias[:, :], bias[:, :], slope_c[:, 0:1], bias_mul[:, 0:1], ALU.mult, ALU.mult
                            ).then_inc(bias_made, 1)
            for k in range(KD):
                dve.wait_ge(wv_turned, k + 1)
                step(v.tensor_scalar(wvr_h[:, k, 0:D], aux[k][:, 0:D], small_up[:, 1:2], None, ALU.mult), 0)
                last = v.scalar_tensor_tensor(wvr_l[:, k, 0:D], aux[k][:, 0:D], small_up[:, 1:2], wvr_h[:, k, 0:D],
                                              ALU.mult, ALU.subtract)
            last.then_inc(ready, 1)
            dve.wait_ge(ready, 2)
            dve.wait_ge(consts_made, 8)
            for s in (aux_read, score_read, pT_lo, s_made, h_read):
                dve.sem_inc(s, 1)
            first_steps = count[0]

            with dve.Fori(0, B) as b:
                count[0] = 0
                at = b * LOOP_STEPS + first_steps

                def norm(g):
                    k = g % 2
                    dve.wait_ge(x_in[k], b * 32 + g // 2 * 16 + 16)
                    for j in range(GT):
                        last = v.bn_stats(stats[:, j, :], xg[k][:, j, 0:D])
                    step(last, at, True)
                    for j in range(GT):
                        last = v.bn_aggr(mv[:, j, :], stats[:, j, :])
                    step(last, at)
                    v.tensor_scalar(var[:, :], mv[:, :, 1], EPS, None, ALU.add).then_inc(var_made, 1)
                    dve.wait_ge(std_made, b * NG + g + 1)
                    step(v.reciprocal(rec[:, :], std[:, :]), at)
                    step(v.tensor_tensor(sq[:, :], rec[:, :], rec[:, :], ALU.mult), at)
                    step(v.scalar_tensor_tensor(sqv[:, :], sq[:, :], -0.5, var[:, :], ALU.mult, ALU.mult), at)
                    step(v.scalar_tensor_tensor(rstd[:, :], sqv[:, :], 1.5, rec[:, :], ALU.add, ALU.mult), at)
                    if g >= 2:
                        dve.wait_ge(slots_out[k], b * (NG // 2 * GT * 16) + g // 2 * (GT * 16))
                    for j in range(GT):
                        last = v.tensor_scalar(xnr[k][:, j, 0:D], xg[k][:, j, 0:D], mv[:, j, 0:1], rstd[:, j:j + 1],
                                               ALU.subtract, ALU.mult)
                    last.then_inc(xn_made, 1)

                def unit(g, n):
                    u = g * UNITS + n
                    a = aux[u % 2]
                    if n < 8:
                        dve.wait_ge(hi_made, b * (NG * 8) + g * 8 + n + 1)
                    if n < 2:
                        cols = xT_h[:, n, g * GTOK:(g + 1) * GTOK]
                        v.scalar_tensor_tensor(xT_l[:, n, g * GTOK:(g + 1) * GTOK], a[:, :], X_UP, cols,
                                               ALU.mult, ALU.subtract).then_inc(aux_read, 1)
                    elif n < 2 + GT:
                        i = g * GT + n - 2
                        v.scalar_tensor_tensor(v_l[:, i, :], a[:, 0:D], ACC_DOWN, v_h[:, i, :],
                                               ALU.mult, ALU.subtract)
                        v.tensor_scalar(logits[:, n - 2, :], a[:, D:D + E], logit_mul[:, 0:1], None, ALU.mult
                                        ).then_inc(aux_read, 1)
                        if n == 1 + GT:
                            choose(g, u)
                    elif n < 8:
                        e = n - 2 - GT
                        v.scalar_tensor_tensor(qT_l[g % 2][:, e, :], a[:, :], ACC_DOWN, qT_h[g % 2][:, e, :],
                                               ALU.mult, ALU.subtract).then_inc(aux_read, 1)
                    else:
                        route(g, u, a)

                def choose(g, u):
                    dve.wait_ge(aux_read, b * NUNIT + u + 2)
                    step(v.tensor_reduce(lmax[:, :], logits[:, :, :], AX.X, ALU.max), at)
                    v.tensor_tensor(below[:, :, :], logits[:, :, :], lmax[:, :].unsqueeze(2).to_broadcast([P, GT, E]),
                                    ALU.subtract).then_inc(below_made, 1)
                    dve.wait_ge(below_made, b * NG + g + 1)
                    step(v.scalar_tensor_tensor(key[:, :, :], below[:, :, :], 0.0, ranks[:, :, :],
                                                ALU.is_equal, ALU.mult), at)
                    step(v.tensor_reduce(kmax[:, :], key[:, :, :], AX.X, ALU.max), at)
                    v.tensor_tensor(chosen[:, :, :], key[:, :, :], kmax[:, :].unsqueeze(2).to_broadcast([P, GT, E]),
                                    ALU.is_equal).then_inc(chosen_made, 1)
                    v.tensor_scalar(limit[:, :], kmax[:, :], -float(CAP), float((E + 1) * CAP), ALU.mult, ALU.add)
                    dve.wait_ge(lexp_made, b * NG + g + 1)
                    step(v.tensor_reduce(lsum[:, :], lexp[:, :, :], AX.X, ALU.add), at)
                    v.reciprocal(xnr[g % 2][:, :, PCOL], lsum[:, :]).then_inc(prob_set, 1)

                def route(g, u, a):
                    dve.wait_ge(aux_full, b * NUNIT + u + 1)
                    step(v.tensor_tensor(place[:, :, :], a[:, 0:GT * E].rearrange("p (j e) -> p j e", j=GT),
                                         taken[:, :].unsqueeze(1).to_broadcast([P, GT, E]), ALU.add), at)
                    v.tensor_tensor(taken[:, :], a[:, GT * E:GT * E + E], taken[:, :], ALU.add).then_inc(aux_read, 1)
                    dve.wait_ge(aux_read, b * NUNIT + u + 2)
                    step(v.tensor_tensor(placed[:, :, :], place[:, :, :], chosen[:, :, :], ALU.mult), at)
                    step(v.tensor_reduce(slot[:, :], placed[:, :, :], AX.X, ALU.add), at)
                    step(v.tensor_tensor(keep[:, :], slot[:, :], limit[:, :], ALU.is_lt), at)
                    step(v.scalar_tensor_tensor(kept[:, :], slot[:, :], -NOWHERE, keep[:, :], ALU.add, ALU.mult), at)
                    v.tensor_scalar(slot_idx[g % 2][:, :], kept[:, :], NOWHERE, None, ALU.add).then_inc(slot_made, 1)

                def score(i, c):
                    n, w = chunk_no(i, c), chunk_blocks(i, c) * P
                    lo = S - P - i * P + c * 512
                    dve.wait_ge(score_full, b * NCHUNK + n + 1)
                    apart(dve)
                    v.tensor_tensor_reduce(sc[:, i % 2, c * 512:c * 512 + w], sc_ps[n % 2][:, 0:w], bias[:, lo:lo + w],
                                           score_mul[:, 0:1], -3e38, ALU.add, ALU.max, cmax[:, i % 2, c:c + 1]
                                           ).then_inc(score_read, 1)
                    if c == chunks(i) - 1:
                        k = i % 2
                        dve.wait_ge(score_read, b * NCHUNK + n + 2)
                        step(v.tensor_reduce(rmax[:, k:k + 1], cmax[:, k, 0:c + 1], AX.X, ALU.max), at)
                        v.tensor_scalar(nbias[:, k:k + 1], rmax[:, k:k + 1], -1.0, LN2_UP, ALU.mult, ALU.add
                                        ).then_inc(nbias_made, 1)

                def low(i, c):
                    n, w = chunk_no(i, c), chunk_blocks(i, c) * P
                    dve.wait_ge(pT_hi, b * NCHUNK + n + 1)
                    v.tensor_tensor(pT_l[:, i % 2, c * 512:c * 512 + w], tr_ps[n % 2][:, 0:w],
                                    pT_h[:, i % 2, c * 512:c * 512 + w], ALU.subtract).then_inc(pT_lo, 1)

                def finish(i):
                    k = i % 2
                    step(v.tensor_reduce(rsum[:, k:k + 1], psums[:, k, 0:chunks(i)], AX.X, ALU.add), at)
                    step(v.reciprocal(rinv[:, k:k + 1], rsum[:, k:k + 1]), at)
                    dve.wait_ge(pv_full, b * NT + i + 1)
                    v.tensor_scalar(xg[i // GT % 2][:, i % GT, D:2 * D], pv_ps[k][:, 0:D], rinv[:, k:k + 1],
                                    value_mul[:, 0:1], ALU.mult, ALU.mult).then_inc(s_made, 1)

                norm(0)
                for n in range(UNITS):
                    unit(0, n)
                score(0, 0)
                for i in range(NT):
                    for nxt, own, _ in steps(i):
                        if nxt is not None:
                            score(i + 1, nxt)
                        if own is not None:
                            low(i, own)
                    finish(i)
                    if norm_after(i):
                        norm(i // GT + 1)
                    for n in units_after(i):
                        unit(i // GT + 1, n)
                    if i == 9:
                        dve.wait_ge(w_in, b * 16 + 16)
                        v.tensor_reduce(wmax[:, bass.ds(b, 1)], raw[:, bass.ds(b, 1), :], AX.XY, ALU.max,
                                        apply_absolute_value=True).then_inc(w_maxed, 1)
                    if i == 10:
                        dve.wait_ge(w_topped, b + 1)
                        scales(wtop[:, :], wexp[:, :], wup[0][:, :], wdn[:, :], at)
                        v.tensor_scalar(ymul[0][:, :], wdn[:, 0:1], wdn[:, 1:2], UNDO, ALU.mult, ALU.mult
                                        ).then_inc(w_scaled, 1)
                    if i in (12, 13):
                        for q in range(2 * (i - 12), 2 * (i - 12) + 2):
                            cols = slice(q * PIECE, (q + 1) * PIECE)
                            dve.wait_ge(w_hi, b * PIECES + q + 1)
                            v.scalar_tensor_tensor(w_l[0][:, bass.ds(b, 1), cols], raw[:, bass.ds(b, 1), cols],
                                                   wup[0][:, bass.ds(b, 1)], w_h[0][:, bass.ds(b, 1), cols],
                                                   ALU.mult, ALU.subtract).then_inc(w_lo, 1)
                for k in range(2):
                    dve.wait_ge(slots_out[k], b * (NG // 2 * GT * 16) + NG // 2 * GT * 16)
                assert count[0] == LOOP_STEPS, count[0]

            att_steps = first_steps + B * LOOP_STEPS

            def take_rows(k):
                v.tensor_scalar(pk[k][:, :], xe[:, :, PCOL], ymul[k][:, 0:1], None, ALU.mult)
                v.tensor_scalar(get_idx[k][:, :], xe[:, :, TCOL], float(T - 1), None, ALU.min)
                v.tensor_copy(put_idx[k][:, :], xe[:, :, TCOL]).then_inc(idx_made, 1)

            def turn_low(e, k, d):
                dve.wait_ge(xe_hi, e * KD + d + 1)
                v.scalar_tensor_tensor(xeT_l[k][:, d, :], aux[d][:, :], X_UP, xeT_h[k][:, d, :],
                                       ALU.mult, ALU.subtract).then_inc(xe_lo, 1)

            dve.wait_ge(xe_in, 16)
            take_rows(0)
            for d in range(KD):
                turn_low(0, 0, d)

            def expert(i, k, more, at):
                e, o = i * 2 + k, 1 - k
                for f in range(NF):
                    if more and f in (0, 1):
                        if f == 0:
                            dve.wait_ge([w_in, w_in_odd][o], i * 16 + (16 if o else 48))
                        last = v.tensor_reduce(wmax[:, f:f + 1], wraw[o][:, f, :], AX.X, ALU.max,
                                               apply_absolute_value=True)
                        if f == 1:
                            last.then_inc(w_maxed, 1)
                    if more and f == 2:
                        dve.wait_ge(w_topped, e + B + 1)
                        scales(wtop[:, :], wexp[:, :], wup[o][:, :], wdn[:, :], at)
                        v.tensor_scalar(ymul[o][:, :], wdn[:, 0:1], wdn[:, 1:2], UNDO, ALU.mult, ALU.mult
                                        ).then_inc(w_scaled, 1)
                    dve.wait_ge(h_hi, e * NF + f + 1)
                    v.tensor_tensor(hid_l[:, f % 2, :], hid[:, f % 2, :], hid_h[:, f % 2, :], ALU.subtract
                                    ).then_inc(h_lo, 1)
                    if more and f in (3, 5):
                        turn_low(e + 1, o, f // 4)
                    if more and f == 6:
                        dve.wait_ge(xe_in, e * 16 + 32)
                        dve.wait_ge(w_scaled, e + B + 1)
                        for j in range(SJ):
                            dve.wait_ge(back_in[j], e * 16 + 16)
                        take_rows(o)
                    if more and f >= 4:
                        for q in range(2 * (f - 4), 2 * (f - 4) + 2):
                            t, cols = q // PIECES, slice(q % PIECES * PIECE, (q % PIECES + 1) * PIECE)
                            dve.wait_ge(w_hi, (e + 1) * 2 * PIECES + q + 1)
                            v.scalar_tensor_tensor(w_l[o][:, t, cols], wraw[o][:, t, cols], wup[o][:, t:t + 1],
                                                   w_h[o][:, t, cols], ALU.mult, ALU.subtract).then_inc(w_lo, 1)

            with dve.Fori(0, E // 2 - 1) as i:
                count[0] = 0
                for k in range(2):
                    expert(i, k, True, i * PAIR_STEPS + att_steps)
                assert count[0] == PAIR_STEPS, count[0]
            count[0] = 0
            expert(E // 2 - 1, 0, True, (E // 2 - 1) * PAIR_STEPS + att_steps)
            expert(E // 2 - 1, 1, False, 0)

        @block.scalar
        def _(act):
            a_ = nc.scalar

            with act.Fori(0, B) as b:
                def norm(g):
                    act.wait_ge(var_made, b * NG + g + 1)
                    a_.activation(std[:, :], var[:, :], ACT.Sqrt).then_inc(std_made, 1)

                def unit(g, n):
                    if n == 8:
                        return
                    u = g * UNITS + n
                    a = aux[u % 2]
                    act.wait_ge(aux_full, b * NUNIT + u + 1)
                    if n < 2:
                        a_.activation(xT_h[:, n, g * GTOK:(g + 1) * GTOK], a[:, :], ACT.Copy, scale=X_UP
                                      ).then_inc(hi_made, 1)
                    elif n < 2 + GT:
                        a_.activation(v_h[:, g * GT + n - 2, :], a[:, 0:D], ACT.Copy, scale=ACC_DOWN
                                      ).then_inc(hi_made, 1)
                        if n == 1 + GT:
                            act.wait_ge(below_made, b * NG + g + 1)
                            a_.activation(lexp[:, :, :], below[:, :, :], ACT.Exp).then_inc(lexp_made, 1)
                    else:
                        a_.activation(qT_h[g % 2][:, n - 2 - GT, :], a[:, :], ACT.Copy, scale=ACC_DOWN
                                      ).then_inc(hi_made, 1)

                def probs(i):
                    k = i % 2
                    act.wait_ge(nbias_made, b * NT + i + 1)
                    for c in range(chunks(i)):
                        cols = slice(c * 512, c * 512 + chunk_blocks(i, c) * P)
                        a_.activation(sc[:, k, cols], sc[:, k, cols], ACT.Exp, bias=nbias[:, k:k + 1],
                                      accum_out=psums[:, k, c:c + 1]).then_inc(exp_made, 1)

                def high(i, c):
                    n, w = chunk_no(i, c), chunk_blocks(i, c) * P
                    act.wait_ge(turned, b * NCHUNK + n + 1)
                    a_.activation(pT_h[:, i % 2, c * 512:c * 512 + w], tr_ps[n % 2][:, 0:w], ACT.Copy
                                  ).then_inc(pT_hi, 1)

                norm(0)
                for n in range(UNITS):
                    unit(0, n)
                probs(0)
                for i in range(NT):
                    for _, own, _ in steps(i):
                        if own is not None:
                            high(i, own)
                    if i + 1 < NT:
                        probs(i + 1)
                    if norm_after(i):
                        norm(i // GT + 1)
                    for n in units_after(i):
                        unit(i // GT + 1, n)
                    if i in (12, 13):
                        for q in range(2 * (i - 12), 2 * (i - 12) + 2):
                            cols = slice(q * PIECE, (q + 1) * PIECE)
                            act.wait_ge(w_scaled, b + 1)
                            a_.activation(w_h[0][:, bass.ds(b, 1), cols], raw[:, bass.ds(b, 1), cols], ACT.Copy,
                                          scale=wup[0][:, bass.ds(b, 1)]).then_inc(w_hi, 1)

            def turn_high(e, k, d):
                act.wait_ge(xe_turned, e * KD + d + 1)
                a_.activation(xeT_h[k][:, d, :], aux[d][:, :], ACT.Copy, scale=X_UP).then_inc(xe_hi, 1)

            for d in range(KD):
                turn_high(0, 0, d)

            def expert(i, k, more):
                e, o = i * 2 + k, 1 - k
                for f in range(NF):
                    act.wait_ge(h_full, e * NF + f + 1)
                    a_.activation(hid[:, f % 2, :], sc_ps[f % 2][:, :], ACT.Relu, scale=ACC_DOWN).then_inc(h_read, 1)
                    act.wait_ge(h_read, e * NF + f + 2)
                    a_.activation(hid_h[:, f % 2, :], hid[:, f % 2, :], ACT.Copy).then_inc(h_hi, 1)
                    if more and f in (3, 5):
                        turn_high(e + 1, o, f // 4)
                    if more and f >= 4:
                        for q in range(2 * (f - 4), 2 * (f - 4) + 2):
                            t, cols = q // PIECES, slice(q % PIECES * PIECE, (q % PIECES + 1) * PIECE)
                            act.wait_ge(w_scaled, e + B + 1)
                            a_.activation(w_h[o][:, t, cols], wraw[o][:, t, cols], ACT.Copy, scale=wup[o][:, t:t + 1]
                                          ).then_inc(w_hi, 1)
                act.wait_ge(idx_made, e + 1)
                for j in range(SJ):
                    act.wait_ge(y_full, e * SJ + j + 1)
                    act.wait_ge(gate_used, e * SJ + j + 1)
                    a_.activation(gate[:, j, :], y_ps[j][:, 0:D], ACT.Silu, scale=pk[k][:, j:j + 1]
                                  ).then_inc(gate_made, 1)

            with act.Fori(0, E // 2 - 1) as i:
                for k in range(2):
                    expert(i, k, True)
            expert(E // 2 - 1, 0, True)
            expert(E // 2 - 1, 1, False)

        @block.tensor
        def _(pe):
            def product(ps, a_h, a_l, b_h, b_l, first, last):
                pe.matmul(ps, a_h, b_h, start=first, stop=False)
                pe.matmul(ps, a_h, b_l, start=False, stop=False)
                return pe.matmul(ps, a_l, b_h, start=False, stop=last)

            pe.wait_ge(small_in, 64)
            pe.wait_ge(consts_made, 8)
            for k in range(KD):
                for j in range(KD):
                    last = pe.transpose(aux[k][:, j * P:(j + 1) * P], wsmall[:, 1, j, k * P:(k + 1) * P], ident[:, :])
                last.then_inc(wv_turned, 1)
            pe.wait_ge(ready, 2)

            with pe.Fori(0, B) as b:
                def unit(g, n):
                    u = g * UNITS + n
                    a = aux[u % 2]
                    pe.wait_ge(aux_read, b * NUNIT + max(u, 1))
                    if n < 2:
                        if n == 0:
                            pe.wait_ge(xn_made, b * NG + g + 1)
                        for j in range(GT):
                            last = pe.transpose(a[:, j * P:(j + 1) * P], xnr[g % 2][:, j, n * P:(n + 1) * P],
                                                ident[:, :])
                    elif n < 2 + GT:
                        if n == 2:
                            pe.wait_ge(aux_read, b * NUNIT + u + 1)
                        rows_ = slice((g * GT + n - 2) * P, (g * GT + n - 1) * P)
                        for d in range(KD):
                            last = product(a[:, 0:D + E], xT_h[:, d, rows_], xT_l[:, d, rows_],
                                           wvr_h[:, d, :], wvr_l[:, d, :], d == 0, d == KD - 1)
                    elif n < 8:
                        e = n - 2 - GT
                        cols = slice(g * GTOK, (g + 1) * GTOK)
                        for d in range(KD):
                            last = product(a[:, :], wqk_h[:, d, e * P:(e + 1) * P], wqk_l[:, d, e * P:(e + 1) * P],
                                           xT_h[:, d, cols], xT_l[:, d, cols], d == 0, d == KD - 1)
                    else:
                        pe.wait_ge(chosen_made, b * NG + g + 1)
                        pe.matmul(a[:, 0:GT * E], before[:, :], chosen[:, :, :], start=True, stop=False,
                                  skip_group_check=True)
                        for j in range(GT - 1):
                            pe.matmul(a[:, (j + 1) * E:GT * E], ones[:, :],
                                      chosen[:, j:j + 1, :].to_broadcast([P, GT - 1 - j, E]),
                                      start=False, stop=False, skip_group_check=True)
                        for j in range(GT):
                            last = pe.matmul(a[:, GT * E:GT * E + E], ones[:, :], chosen[:, j, :], start=False,
                                             stop=j == GT - 1, skip_group_check=True)
                    last.then_inc(aux_full, 1)

                def score(i, c):
                    n, w, g = chunk_no(i, c), chunk_blocks(i, c) * P, i // GT
                    if c == 0 and i % GT == 0:
                        pe.wait_ge(aux_read, b * NUNIT + g * UNITS + 9)
                    pe.wait_ge(score_read, b * NCHUNK + max(n, 1))
                    rows_, cols = slice(i % GT * P, (i % GT + 1) * P), slice(c * 512, c * 512 + w)
                    for d in range(KD):
                        last = product(sc_ps[n % 2][:, 0:w], qT_h[g % 2][:, d, rows_], qT_l[g % 2][:, d, rows_],
                                       xT_h[:, d, cols], xT_l[:, d, cols], d == 0, d == KD - 1)
                    last.then_inc(score_full, 1)

                def turn(i, c):
                    n = chunk_no(i, c)
                    pe.wait_ge(exp_made, b * NCHUNK + n + 1)
                    pe.wait_ge(pT_lo, b * NCHUNK + max(n, 1))
                    for q in range(chunk_blocks(i, c)):
                        col = c * 512 + q * P
                        last = pe.transpose(tr_ps[n % 2][:, q * P:(q + 1) * P], sc[:, i % 2, col:col + P], ident[:, :])
                    last.then_inc(turned, 1)

                def values(i, c):
                    n = chunk_no(i, c)
                    pe.wait_ge(pT_lo, b * NCHUNK + n + 2)
                    if c == 0:
                        pe.wait_ge(s_made, b * NT + max(i, 1))
                    for q in range(chunk_blocks(i, c)):
                        kb = c * GT + q
                        rows_ = slice(kb * P, (kb + 1) * P)
                        last = product(pv_ps[i % 2][:, 0:D], pT_h[:, i % 2, rows_], pT_l[:, i % 2, rows_],
                                       v_h[:, kb, :], v_l[:, kb, :], kb == 0, kb == i)
                    if c == chunks(i) - 1:
                        last.then_inc(pv_full, 1)

                for n in range(UNITS):
                    unit(0, n)
                score(0, 0)
                for i in range(NT):
                    for nxt, own, val in steps(i):
                        if nxt is not None:
                            score(i + 1, nxt)
                        if own is not None:
                            turn(i, own)
                        if val is not None:
                            values(i, val)
                    for n in units_after(i):
                        unit(i // GT + 1, n)

            def turn_rows(e, d):
                if d == 0:
                    pe.wait_ge(xe_in, e * 16 + 16)
                for j in range(SJ):
                    last = pe.transpose(aux[d][:, j * P:(j + 1) * P], xe[:, j, d * P:(d + 1) * P], ident[:, :])
                last.then_inc(xe_turned, 1)

            pe.wait_ge(aux_read, B * NUNIT + 1)
            pe.wait_ge(s_made, B * NT + 1)
            for d in range(KD):
                turn_rows(0, d)

            def expert(i, k, more):
                e, o = i * 2 + k, 1 - k

                def up(f):
                    if f == 0:
                        pe.wait_ge(w_lo, (e + 1) * 2 * PIECES)
                        pe.wait_ge(xe_lo, e * KD + KD)
                    pe.wait_ge(h_read, e * NF + max(f, 1))
                    for d in range(KD):
                        rows_ = slice(d * F + f * P, d * F + (f + 1) * P)
                        last = product(sc_ps[f % 2][:, :], w_h[k][:, 0, rows_], w_l[k][:, 0, rows_],
                                       xeT_h[k][:, d, :], xeT_l[k][:, d, :], d == 0, d == KD - 1)
                    last.then_inc(h_full, 1)

                def down(f):
                    pe.wait_ge(h_lo, e * NF + f + 1)
                    if f == 0:
                        pe.wait_ge(gate_made, e * SJ + SJ)
                    cols = slice(f * D, (f + 1) * D)
                    for j in range(SJ):
                        rows_ = slice(j * P, (j + 1) * P)
                        last = product(y_ps[j][:, 0:D], hid_h[:, f % 2, rows_], hid_l[:, f % 2, rows_],
                                       w_h[k][:, 1, cols], w_l[k][:, 1, cols], f == 0, f == NF - 1)
                        if f == NF - 1:
                            last.then_inc(y_full, 1)

                up(0)
                for f in range(NF):
                    if f + 1 < NF:
                        up(f + 1)
                    if more and f in (3, 5):
                        pe.wait_ge(xe_lo, e * KD + f // 4 + 1)
                        turn_rows(e + 1, f // 4)
                    down(f)

            with pe.Fori(0, E // 2 - 1) as i:
                for k in range(2):
                    expert(i, k, True)
            expert(E // 2 - 1, 0, True)
            expert(E // 2 - 1, 1, False)


_INS = ["L0_attn_x", "L0_attn_W_qk", "L0_attn_W_v", "L0_attn_alibi_slope", "L0_ffn_Wr"]


def kernel(**inputs):
    import numpy as np
    import concourse.bacc as bacc
    from concourse.bass_utils import run_bass_kernel_spmd

    def plain(name):
        return np.ascontiguousarray(np.asarray(inputs[name]))

    w1 = plain("L0_ffn_W1").reshape(E, KD, P, F).transpose(0, 2, 1, 3).reshape(E, P, WCOLS)
    w2 = plain("L0_ffn_W2").reshape(E, NF, P, D).transpose(0, 2, 1, 3).reshape(E, P, WCOLS)
    arrays = {
        "in_x": plain("L0_attn_x").reshape(T, D), "in_w_qk": plain("L0_attn_W_qk"), "in_w_v": plain("L0_attn_W_v"),
        "in_slope": plain("L0_attn_alibi_slope"), "in_w_r": plain("L0_ffn_Wr"),
        "in_w_e": np.ascontiguousarray(np.stack([w1, w2], axis=1)),
    }
    nc = bacc.Bacc("TRN2", target_bir_lowering=False, num_devices=1)
    args = [nc.dram_tensor(n, a.shape, mybir.dt.from_np(a.dtype), kind="ExternalInput").ap()
            for n, a in arrays.items()]
    args.append(nc.dram_tensor("out_0", (T, D), F32, kind="ExternalOutput").ap())
    args.append(nc.dram_tensor("slots", (T, ROW), F32).ap())
    args.append(nc.dram_tensor("rows", (T, 2 * D), F32).ap())
    layer_kernel(nc, *args)
    r = run_bass_kernel_spmd(nc, [arrays], core_ids=[0])
    return r.results[0]["out_0"].reshape(B, S, D)
```

```python
from contextlib import ExitStack

import concourse.bass as bass
from concourse import mybir

P = 128
B, S, D = 2, 2048, 256
E, F = 8, 1024
T = B * S
CAP = T // E
KD = D // P
NT = S // P
TILES = B * NT
GT = 4
GTOK = GT * P
NG = NT // GT
GROUPS = B * NG
NF = F // P
SJ = CAP // P
ROW = D + 8
PCOL, TCOL = D, D + 1
NOWHERE = float(1 << 20)
PIECE = 512
WCOLS = KD * F
PIECES = WCOLS // PIECE

X_UP = 2.0 ** 10
ACC_DOWN = 2.0 ** -18
W_TOP = 14
UNDO = 2.0 ** 8
SM_SCALE = 2.0 ** -4
LN2_UP = 14 * 0.6931471805599453
EPS = 1e-5

HALVED = 8
XT, VAL, QRY = 0, KD, KD + GT
RANK = HALVED
UNITS = HALVED + 1
PAIR_STEPS = 2 * 5
HB = 4
LEAD = 2
TURN_AT = (1, 3)
SPLIT_AT = {1: (0,), 2: (1, 2), 3: (3,), 4: (4, 5), 5: (6, 7)}
MAX_AT = {5: (0,), 6: (1, 2, 3), 7: (4, 5, 6, 7)}

F32 = mybir.dt.float32
F16 = mybir.dt.float16
I32 = mybir.dt.int32
U32 = mybir.dt.uint32
ALU = mybir.AluOpType
ACT = mybir.ActivationFunctionType
AX = mybir.AxisListType
RMAX = bass.bass_isa.ReduceOp.absmax


def chunks(t):
    return t % NT // GT + 1 if 0 <= t < TILES else 0


def chunk_no(t, c):
    return sum(chunks(k) for k in range(t)) + c


def chunk_blocks(t, c):
    return GT if c < chunks(t) - 1 else t % GT + 1


def key_slot(b, g):
    return g if g else b * NG


ALL_CHUNKS = sum(chunks(t) for t in range(TILES))


def layer_kernel(nc, x, w_qk, w_v, slope, w_r, w_e, out, slots, rows):
    with ExitStack() as ctx:
        def sb(name, shape, dt=F32):
            return ctx.enter_context(nc.sbuf_tensor(name, shape, dt))

        def sem(name):
            return ctx.enter_context(nc.semaphore(name))

        ident = sb("ident", [P, P])
        before = sb("before", [P, P], F16)
        ones = sb("ones", [P, P], F16)
        ranks = sb("ranks", [P, GT, E])
        bias = sb("bias", [P, S])
        slope_c = sb("slope_c", [P, 1])
        wqk_h = sb("wqk_h", [P, KD, D], F16)
        wqk_l = sb("wqk_l", [P, KD, D], F16)
        wvr_h = sb("wvr_h", [P, KD, D + E], F16)
        wvr_l = sb("wvr_l", [P, KD, D + E], F16)
        small_max = sb("small_max", [P, 3])
        small_top = sb("small_top", [P, 3])
        small_exp = sb("small_exp", [P, 3])
        small_up = sb("small_up", [P, 3])
        small_dn = sb("small_dn", [P, 3])
        score_mul = sb("score_mul", [P, 1])
        bias_mul = sb("bias_mul", [P, 1])
        value_mul = sb("value_mul", [P, 1])
        logit_mul = sb("logit_mul", [P, 1])
        empty = sb("empty", [P, ROW])

        xg = [sb(f"xg{k}", [P, GT, D]) for k in range(2)]
        so = [sb(f"so{k}", [P, GT, D]) for k in range(2)]
        xnr = [sb(f"xnr{k}", [P, GT, ROW]) for k in range(2)]
        stats = sb("stats", [P, GT, 6])
        mv = sb("mv", [P, GT, 2])
        var = sb("var", [P, GT])
        power = sb("power", [P, GT])
        rec = sb("rec", [P, GT])
        sq = sb("sq", [P, GT])
        sqv = sb("sqv", [P, GT])
        rstd = sb("rstd", [P, GT])
        xT_h = sb("xT_h", [P, KD, NG + 1, GTOK], F16)
        xT_l = sb("xT_l", [P, KD, NG + 1, GTOK], F16)
        v_h = sb("v_h", [P, NG + 1, GT, D], F16)
        v_l = sb("v_l", [P, NG + 1, GT, D], F16)
        qT_h = [sb(f"qT_h{k}", [P, KD, GTOK], F16) for k in range(2)]
        qT_l = [sb(f"qT_l{k}", [P, KD, GTOK], F16) for k in range(2)]
        logits = sb("logits", [P, GT, E])
        lmax = sb("lmax", [P, GT])
        below = sb("below", [P, GT, E])
        lexp = sb("lexp", [P, GT, E])
        lsum = sb("lsum", [P, GT])
        key = sb("key", [P, GT, E])
        kmax = sb("kmax", [P, GT])
        chosen = sb("chosen", [P, GT, E], F16)
        place = sb("place", [P, GT, E])
        placed = sb("placed", [P, GT, E])
        slot = sb("slot", [P, GT])
        limit = sb("limit", [P, GT])
        keep = sb("keep", [P, GT])
        kept = sb("kept", [P, GT])
        slot_idx = [sb(f"slot_idx{k}", [P, GT], U32) for k in range(2)]
        taken = sb("taken", [P, E])
        token = sb("token", [P, GT])

        sc = sb("sc", [P, 2, S])
        cmax = sb("cmax", [P, 2, NG])
        rmax = sb("rmax", [P, 2])
        nbias = sb("nbias", [P, 2])
        psums = sb("psums", [P, 3, NG])
        rsum = sb("rsum", [P, 2])
        rinv = sb("rinv", [P, 2])
        pT_h = sb("pT_h", [P, 2, S], F16)
        pT_l = sb("pT_l", [P, 2, S], F16)
        wsmall = sc[:, 1, 0:3 * KD * D].rearrange("p (a k n) -> p a k n", a=3, k=KD)

        raw = sb("raw", [P, 2, WCOLS])
        wraw = [sc, raw]
        w_h = [sb(f"w_h{k}", [P, 2, WCOLS], F16) for k in range(2)]
        w_l = [sb(f"w_l{k}", [P, 2, WCOLS], F16) for k in range(2)]
        pmax = sb("pmax", [P, 2, PIECES])
        wmax = sb("wmax", [P, 2])
        wtop = sb("wtop", [P, 2])
        wexp = sb("wexp", [P, 2])
        wup = [sb(f"wup{k}", [P, 2]) for k in range(2)]
        wdn = sb("wdn", [P, 2])
        ymul = [sb(f"ymul{k}", [P, 1]) for k in range(2)]
        xe = sb("xe", [P, SJ, ROW])
        xeT_h = [sb(f"xeT_h{k}", [P, KD, CAP], F16) for k in range(2)]
        xeT_l = [sb(f"xeT_l{k}", [P, KD, CAP], F16) for k in range(2)]
        pk = [sb(f"pk{k}", [P, SJ]) for k in range(2)]
        get_idx = [sb(f"get_idx{k}", [P, SJ], U32) for k in range(2)]
        put_idx = [sb(f"put_idx{k}", [P, SJ], U32) for k in range(2)]
        hid = sb("hid", [P, 2, CAP])
        hid_h = sb("hid_h", [P, HB, CAP], F16)
        hid_l = sb("hid_l", [P, HB, CAP], F16)
        gate = sb("gate", [P, SJ, D])
        back = [sb(f"back{j}", [P, 2 * D]) for j in range(SJ)]
        warm = sb("warm", [P, 1])

        bank = [ctx.enter_context(nc.psum_tensor(f"bank{k}", [P, 512], F32)) for k in range(8)]
        sc_ps, tr_ps, pv_ps, aux = bank[0:2], bank[2:4], bank[4:6], bank[6:8]
        y_ps = [[bank[2 + 2 * k + j // 2][:, j % 2 * D:(j % 2 + 1) * D] for j in range(SJ)] for k in range(2)]

        x_in = [sem(f"x_in{k}") for k in range(2)]
        small_in = sem("small_in")
        slots_empty = sem("slots_empty")
        out_first = [sem(f"out_first{k}") for k in range(2)]
        rows_x = [sem(f"rows_x{k}") for k in range(2)]
        rows_s = [sem(f"rows_s{k}") for k in range(2)]
        slots_out = [sem(f"slots_out{k}") for k in range(2)]
        w_in = [sem("w_in_sc"), sem("w_in_raw")]
        xe_in = sem("xe_in")
        back_in = [sem(f"back_in{j}") for j in range(SJ)]
        out_put = [sem(f"out_put{j}") for j in range(SJ)]
        consts_made = sem("consts_made")
        small_maxed = sem("small_maxed")
        small_topped = sem("small_topped")
        wv_turned = sem("wv_turned")
        bias_made = sem("bias_made")
        masked = sem("masked")
        small_scaled = sem("small_scaled")
        small_hi = sem("small_hi")
        values_ready = sem("values_ready")
        ready = sem("ready")
        bias_raw = sem("bias_raw")
        pool_step = sem("pool_step")
        dve_step = sem("dve_step")
        var_made = sem("var_made")
        rec_made = sem("rec_made")
        xn_made = sem("xn_made")
        aux_full = sem("aux_full")
        aux_read = sem("aux_read")
        hi_made = sem("hi_made")
        below_made = sem("below_made")
        lexp_made = sem("lexp_made")
        chosen_made = sem("chosen_made")
        token_set = sem("token_set")
        prob_set = sem("prob_set")
        slot_made = sem("slot_made")
        score_full = sem("score_full")
        score_read = sem("score_read")
        nbias_made = sem("nbias_made")
        exp_made = sem("exp_made")
        turned = sem("turned")
        pT_hi = sem("pT_hi")
        pT_lo = sem("pT_lo")
        pv_full = sem("pv_full")
        s_made = sem("s_made")
        w_maxed = sem("w_maxed")
        w_topped = sem("w_topped")
        w_scaled = sem("w_scaled")
        w_hi = sem("w_hi")
        w_lo = sem("w_lo")
        xe_turned = sem("xe_turned")
        xe_hi = sem("xe_hi")
        xe_lo = sem("xe_lo")
        idx_made = sem("idx_made")
        h_full = sem("h_full")
        h_read = sem("h_read")
        h_hi = sem("h_hi")
        h_lo = sem("h_lo")
        y_full = sem("y_full")
        gate_made = sem("gate_made")
        gated = sem("gated")
        done_made = sem("done_made")
        put_over = sem("put_over")
        passed = sem("passed")

        x_g = x.rearrange("(g j p) d -> g p j d", p=P, j=GT)
        out_g = out.rearrange("(g j p) d -> g p j d", p=P, j=GT)
        rows_g = rows.rearrange("(g j p) d -> g p j d", p=P, j=GT)
        slots_e = slots.rearrange("(e j p) d -> e p j d", p=P, j=SJ)
        w_k = w_e.rearrange("e k p n -> e p k n")

        block = ctx.enter_context(nc.Block())

        def steps(t):
            return range(max(chunks(t + 1), chunks(t), chunks(t - 1)))

        def last_step(t, c):
            return c == len(steps(t)) - 1

        def units_after(t, c):
            g, j = t // GT + 1, t % GT
            first, last = c == 0, last_step(t, c)
            if g == GROUPS:
                return []
            if j == 0:
                return [XT, XT + 1] * first + [VAL, VAL + 1] * last
            if j == 1:
                return [VAL + 2, VAL + 3, QRY] * last
            return [QRY + 1] * first if j == 2 else [RANK] * first

        FIRST_MAX, FIRST_SCALE, FIRST_SPLIT = (4, 5, 6, 7), 8, (9, 10, 11, 12, 13, 14, 15, 16)
        SECOND_MAX = (22, 23, 24, 25, 26, 27, 28, 29)
        FIRST_ROWS = TILES - 2

        def share(tiles, t):
            n = 2 * PIECES // len(tiles)
            return range(tiles.index(t) * n, (tiles.index(t) + 1) * n) if t in tiles else ()

        def piece(q):
            return q // PIECES, slice(q % PIECES * PIECE, (q % PIECES + 1) * PIECE)

        def apart(eng):
            eng.sem_inc(passed, 1)

        @block.sync
        def _(sp):
            sp.dma_start(wsmall[:, 0], w_qk.rearrange("(k p) n -> p k n", p=P)).then_inc(small_in, 16)
            sp.dma_start(wsmall[:, 1], w_v.rearrange("(k p) n -> p k n", p=P)).then_inc(small_in, 16)
            sp.dma_start(wsmall[:, 2, :, 0:E], w_r.rearrange("(k p) n -> p k n", p=P)).then_inc(small_in, 16)
            sp.dma_start(slope_c[:, :], slope.rearrange("(o n) -> o n", o=1).partition_broadcast(P)
                         ).then_inc(small_in, 16)
            sp.dma_start(xg[1][:, :, :], x_g[1]).then_inc(x_in[1], 16)
            sp.wait_ge(consts_made, 1)
            sp.dma_start(slots.rearrange("(k p) r -> p k r", p=P),
                         empty[:, :].unsqueeze(1).to_broadcast([P, T // P, ROW])).then_inc(slots_empty, 16)
            sp.dma_start(raw[:, :, :], w_k[0]).then_inc(w_in[1], 16)
            for g in range(GROUPS):
                k, n = g % 2, (g // 2 + 1) * 16
                sp.wait_ge(x_in[k], n)
                sp.dma_start(out_g[g], xg[k][:, :, :]).then_inc(out_first[k], 16)
                sp.dma_start(rows_g[g][:, :, 0:D], xg[k][:, :, :]).then_inc(rows_x[k], 16)
                if g + 2 < GROUPS:
                    sp.wait_ge(xn_made, g + 1)
                    sp.wait_ge(out_first[k], n)
                    sp.wait_ge(rows_x[k], n)
                    sp.dma_start(xg[k][:, :, :], x_g[g + 2]).then_inc(x_in[k], 16)
                if g > 0:
                    sp.wait_ge(s_made, g * GT)
                    sp.dma_start(rows_g[g - 1][:, :, D:2 * D], so[1 - k][:, :, :]).then_inc(rows_s[1 - k], 16)
                if g == NG:
                    sp.wait_ge(w_lo, 2 * PIECES)
                    sp.dma_start(raw[:, :, :], w_k[1]).then_inc(w_in[1], 16)
            for k in range(2):
                sp.wait_ge(slots_out[k], GROUPS // 2 * GT * 16)
            sp.dma_start(xe[:, :, :], slots_e[0]).then_inc(xe_in, 16)
            sp.wait_ge(turned, ALL_CHUNKS)
            sp.dma_start(sc[:, :, :], w_k[2]).then_inc(w_in[0], 16)
            sp.wait_ge(s_made, TILES)
            sp.dma_start(rows_g[GROUPS - 1][:, :, D:2 * D], so[1][:, :, :]).then_inc(rows_s[1], 16)

            def next_rows(e):
                sp.wait_ge(xe_turned, e * KD)
                sp.wait_ge(idx_made, e)
                sp.dma_start(xe[:, :, :], slots_e[e] if isinstance(e, int) else slots_e[bass.ds(e, 1)]
                             ).then_inc(xe_in, 16)

            def next_weights(e, k):
                sp.wait_ge(w_lo, (e - 1) * 2 * PIECES)
                sp.dma_start(wraw[k][:, :, :], w_k[e] if isinstance(e, int) else w_k[bass.ds(e, 1)]
                             ).then_inc(w_in[k], 16)

            next_rows(1)
            with sp.Fori(0, (E - 4) // 2) as i:
                for k in range(2):
                    next_rows(i * 2 + k + 2)
                    next_weights(i * 2 + k + 3, 1 - k)
            next_rows(E - 2)
            next_weights(E - 1, 1)
            next_rows(E - 1)

        @block.gpsimd
        def _(pool):
            g_ = nc.gpsimd
            g_.memset(empty[:, :], 0.0).then_inc(pool_step, 1)
            pool.wait_ge(pool_step, 1)
            g_.memset(empty[:, TCOL:TCOL + 1], NOWHERE).then_inc(consts_made, 1)
            g_.memset(ident[:, :], 0.0).then_inc(pool_step, 1)
            g_.memset(ones[:, :], 1.0).then_inc(pool_step, 1)
            pool.wait_ge(pool_step, 3)
            g_.affine_select(out=ident[:, :], in_=ident[:, :], compare_op=ALU.not_equal, fill=1.0, base=0,
                             pattern=[[-1, P]], channel_multiplier=1).then_inc(consts_made, 1)
            g_.affine_select(out=before[:, :], in_=ones[:, :], compare_op=ALU.is_gt, fill=0.0, base=0,
                             pattern=[[1, P]], channel_multiplier=-1).then_inc(consts_made, 1)
            g_.iota(ranks[:, :, :], pattern=[[0, GT], [-1, E]], base=E, channel_multiplier=0,
                    allow_small_or_imprecise_dtypes=True).then_inc(consts_made, 1)
            g_.iota(taken[:, :], pattern=[[CAP, E]], base=0, channel_multiplier=0,
                    allow_small_or_imprecise_dtypes=True).then_inc(consts_made, 1)
            g_.iota(token[:, :], pattern=[[P, GT]], base=0, channel_multiplier=1,
                    allow_small_or_imprecise_dtypes=True).then_inc(consts_made, 1)
            g_.memset(power[:, :], -0.5).then_inc(pool_step, 1)
            for k in range(2):
                g_.memset(xnr[k][:, :, D:ROW], 0.0).then_inc(consts_made, 1)
            g_.iota(bias[:, :], pattern=[[1, S]], base=P - S, channel_multiplier=-1,
                    allow_small_or_imprecise_dtypes=True).then_inc(bias_raw, 1)

            def inverse(g):
                pool.wait_ge(var_made, g + 1)
                g_.tensor_tensor(rec[:, :], var[:, :], power[:, :], ALU.pow).then_inc(rec_made, 1)

            pool.wait_ge(small_maxed, 1)
            g_.partition_all_reduce(small_top[:, :], small_max[:, :], P, RMAX).then_inc(small_topped, 1)
            pool.wait_ge(pool_step, 4)
            inverse(0)
            pool.wait_ge(bias_made, 1)
            g_.affine_select(out=bias[:, S - P:S], in_=bias[:, S - P:S], compare_op=ALU.is_ge, fill=-3e38,
                             base=0, pattern=[[-1, P]], channel_multiplier=1).then_inc(masked, 1)
            pool.sem_inc(gate_made, 2 * SJ)
            pool.sem_inc(done_made, SJ)
            pool.sem_inc(put_over, 1)
            pool.wait_ge(slots_empty, 16)

            def top(e):
                pool.wait_ge(w_maxed, e + 1)
                apart(pool)
                g_.partition_all_reduce(wtop[:, :], wmax[:, :], P, RMAX).then_inc(w_topped, 1)

            for g in range(GROUPS):
                k = g % 2
                if g + 1 < GROUPS:
                    inverse(g + 1)
                pool.wait_ge(xn_made, g + 1)
                g_.tensor_copy(xnr[k][:, :, TCOL], token[:, :]).then_inc(token_set, 1)
                pool.wait_ge(token_set, g + 1)
                g_.tensor_scalar(token[:, :], token[:, :], float(GTOK), None, ALU.add).then_inc(pool_step, 1)
                pool.wait_ge(pool_step, g + 5)
                pool.wait_ge(prob_set, g + 1)
                pool.wait_ge(slot_made, g + 1)
                for j in range(GT):
                    g_.indirect_dma_start(
                        slots[:, :], bass.IndirectOffsetOnAxis(ap=slot_idx[k][:, j:j + 1], axis=0),
                        xnr[k][:, j, :], None, bounds_check=T - 1, oob_is_err=False).then_inc(slots_out[k], 16)
                if g == FIRST_MAX[0] // GT + 1:
                    top(0)
            top(1)

            def fetch(e, k, j):
                g_.indirect_dma_start(
                    back[j][:, :], None, rows[:, :],
                    bass.IndirectOffsetOnAxis(ap=get_idx[k][:, j:j + 1], axis=0)).then_inc(back_in[j], 16)

            for k in range(2):
                pool.wait_ge(rows_s[k], GROUPS // 2 * 16)
                pool.wait_ge(rows_x[k], GROUPS // 2 * 16)
                pool.wait_ge(out_first[k], GROUPS // 2 * 16)
            pool.wait_ge(idx_made, 1)
            for j in range(SJ):
                fetch(0, 0, j)

            def put(e, k, j):
                pool.wait_ge(done_made, e * SJ + j + 1 + SJ)
                apart(pool)
                g_.indirect_dma_start(
                    out[:, :], bass.IndirectOffsetOnAxis(ap=put_idx[k][:, j:j + 1], axis=0),
                    back[j][:, 0:D], None, bounds_check=T - 1, oob_is_err=False).then_inc(out_put[j], 16)

            def expert(e, k, far):
                if far:
                    top(e + 2)
                for j in range(SJ):
                    pool.wait_ge(gate_made, e * SJ + j + 1 + 2 * SJ)
                    pool.wait_ge(back_in[j], e * 16 + 16)
                    g_.tensor_tensor(gate[:, j, :], gate[:, j, :], back[j][:, D:2 * D], ALU.mult).then_inc(gated, 1)
                    pool.wait_ge(gated, e * SJ + j + 1)
                    g_.tensor_tensor(back[j][:, 0:D], gate[:, j, :], back[j][:, 0:D], ALU.add).then_inc(done_made, 1)
                    put(e, k, j)
                for j in range(SJ):
                    pool.wait_ge(out_put[j], e * 16 + 16)
                pool.sem_inc(put_over, 1)
                pool.wait_ge(idx_made, e + 2)
                apart(pool)
                for j in range(SJ):
                    fetch(e + 1, 1 - k, j)

            with pool.Fori(0, E // 2 - 1) as i:
                for k in range(2):
                    expert(i * 2 + k, k, True)
            expert(E - 2, 0, False)
            for j in range(SJ):
                put(E - 1, 1, j)
            for j in range(SJ):
                pool.wait_ge(out_put[j], 16 * E)

        @block.vector
        def _(dve):
            v = nc.vector
            count = [0]

            def step(ins, at=0, alone=False):
                count[0] += 1
                ins.then_inc(dve_step, 1)
                dve.wait_ge(dve_step, at + count[0])

            def norm_stats(g):
                k = g % 2
                dve.wait_ge(x_in[k], (g // 2 + 1) * 16)
                for j in range(GT):
                    last = v.bn_stats(stats[:, j, :], xg[k][:, j, :])
                step(last)
                for j in range(GT):
                    last = v.bn_aggr(mv[:, j, :], stats[:, j, :])
                step(last)
                v.tensor_scalar(var[:, :], mv[:, :, 1], EPS, None, ALU.add).then_inc(var_made, 1)

            def norm_scale(g):
                dve.wait_ge(rec_made, g + 1)
                step(v.tensor_tensor(sq[:, :], rec[:, :], rec[:, :], ALU.mult))
                step(v.scalar_tensor_tensor(sqv[:, :], sq[:, :], -0.5, var[:, :], ALU.mult, ALU.mult))
                step(v.scalar_tensor_tensor(rstd[:, :], sqv[:, :], 1.5, rec[:, :], ALU.add, ALU.mult))

            def norm_rows(g):
                k = g % 2
                if g >= 2:
                    dve.wait_ge(slots_out[k], g // 2 * GT * 16)
                for j in range(GT):
                    last = v.tensor_scalar(xnr[k][:, j, 0:D], xg[k][:, j, :], mv[:, j, 0:1], rstd[:, j:j + 1],
                                           ALU.subtract, ALU.mult)
                last.then_inc(xn_made, 1)

            dve.wait_ge(small_in, 64)
            v.tensor_reduce(small_max[:, 0:1], wsmall[:, 0], AX.XY, ALU.max, apply_absolute_value=True)
            v.tensor_reduce(small_max[:, 1:2], wsmall[:, 1], AX.XY, ALU.max, apply_absolute_value=True)
            v.tensor_reduce(small_max[:, 2:3], wsmall[:, 2, :, 0:E], AX.XY, ALU.max, apply_absolute_value=True
                            ).then_inc(small_maxed, 1)

            def scales(top, exp, up, dn, at=0):
                step(v.tensor_scalar(exp, top, 2.0 ** -100, None, ALU.max), at)
                step(v.tensor_scalar(exp.bitcast(I32), exp.bitcast(I32), 0x7F800000, None, ALU.bitwise_and), at)
                step(v.tensor_scalar(up.bitcast(I32), exp.bitcast(I32), float((2 * 127 + W_TOP) << 23), -1.0,
                                     ALU.subtract, ALU.mult), at)
                step(v.tensor_scalar(dn.bitcast(I32), exp.bitcast(I32), float(W_TOP << 23), None, ALU.subtract), at)

            norm_stats(0)
            dve.wait_ge(small_topped, 1)
            scales(small_top[:, :], small_exp[:, :], small_up[:, :], small_dn[:, :])
            v.tensor_scalar(score_mul[:, :], small_dn[:, 0:1], SM_SCALE * UNDO / X_UP, None, ALU.mult)
            v.tensor_scalar(value_mul[:, :], small_dn[:, 1:2], UNDO, None, ALU.mult)
            v.tensor_scalar(logit_mul[:, :], small_dn[:, 2:3], 1.0 / X_UP, None, ALU.mult)
            v.tensor_scalar(bias_mul[:, :], small_up[:, 0:1], X_UP / (SM_SCALE * UNDO), None, ALU.mult
                            ).then_inc(small_scaled, 1)
            dve.wait_ge(consts_made, 8)
            norm_scale(0)
            norm_rows(0)
            dve.wait_ge(small_hi, 1)
            v.scalar_tensor_tensor(wvr_l[:, :, D:D + E], wsmall[:, 2, :, 0:E], small_up[:, 2:3],
                                   wvr_h[:, :, D:D + E], ALU.mult, ALU.subtract)
            for k in range(KD):
                dve.wait_ge(small_hi, 2 + k)
                last = v.scalar_tensor_tensor(wvr_l[:, k, 0:D], tr_ps[k][:, 0:D], small_up[:, 1:2], wvr_h[:, k, 0:D],
                                              ALU.mult, ALU.subtract)
            last.then_inc(values_ready, 1)

            def query_weights():
                dve.wait_ge(small_hi, 2 + KD)
                v.scalar_tensor_tensor(wqk_l[:, :, :], wsmall[:, 0], small_up[:, 0:1], wqk_h[:, :, :],
                                       ALU.mult, ALU.subtract).then_inc(ready, 1)

            def bias_table():
                dve.wait_ge(bias_raw, 1)
                v.tensor_scalar(bias[:, :], bias[:, :], slope_c[:, 0:1], bias_mul[:, 0:1], ALU.mult, ALU.mult
                                ).then_inc(bias_made, 1)

            def unit(g, n):
                u = g * UNITS + n
                a, at = aux[u % 2], key_slot(g // NG, g % NG)
                if n < HALVED:
                    dve.wait_ge(hi_made, g * HALVED + n + 1)
                if n < VAL:
                    v.scalar_tensor_tensor(xT_l[:, n, at, :], a[:, :], X_UP, xT_h[:, n, at, :],
                                           ALU.mult, ALU.subtract).then_inc(aux_read, 1)
                elif n < QRY:
                    j = n - VAL
                    v.scalar_tensor_tensor(v_l[:, at, j, :], a[:, 0:D], ACC_DOWN, v_h[:, at, j, :],
                                           ALU.mult, ALU.subtract)
                    v.tensor_scalar(logits[:, j, :], a[:, D:D + E], logit_mul[:, 0:1], None, ALU.mult
                                    ).then_inc(aux_read, 1)
                    if j == GT - 1:
                        choose(g, u)
                elif n < RANK:
                    v.scalar_tensor_tensor(qT_l[g % 2][:, n - QRY, :], a[:, :], ACC_DOWN, qT_h[g % 2][:, n - QRY, :],
                                           ALU.mult, ALU.subtract).then_inc(aux_read, 1)
                else:
                    route(g, u, a)

            def choose(g, u):
                dve.wait_ge(aux_read, u + 1)
                step(v.tensor_reduce(lmax[:, :], logits[:, :, :], AX.X, ALU.max))
                v.tensor_tensor(below[:, :, :], logits[:, :, :], lmax[:, :].unsqueeze(2).to_broadcast([P, GT, E]),
                                ALU.subtract).then_inc(below_made, 1)
                dve.wait_ge(below_made, g + 1)
                step(v.scalar_tensor_tensor(key[:, :, :], below[:, :, :], 0.0, ranks[:, :, :],
                                            ALU.is_equal, ALU.mult))
                step(v.tensor_reduce(kmax[:, :], key[:, :, :], AX.X, ALU.max))
                v.tensor_tensor(chosen[:, :, :], key[:, :, :], kmax[:, :].unsqueeze(2).to_broadcast([P, GT, E]),
                                ALU.is_equal).then_inc(chosen_made, 1)
                v.tensor_scalar(limit[:, :], kmax[:, :], -float(CAP), float((E + 1) * CAP), ALU.mult, ALU.add)
                dve.wait_ge(lexp_made, g + 1)
                step(v.tensor_reduce(lsum[:, :], lexp[:, :, :], AX.X, ALU.add))
                v.reciprocal(xnr[g % 2][:, :, PCOL], lsum[:, :]).then_inc(prob_set, 1)

            def route(g, u, a):
                dve.wait_ge(aux_full, u + 1)
                step(v.tensor_tensor(place[:, :, :], a[:, 0:GT * E].rearrange("p (j e) -> p j e", j=GT),
                                     taken[:, :].unsqueeze(1).to_broadcast([P, GT, E]), ALU.add))
                v.tensor_tensor(taken[:, :], a[:, GT * E:GT * E + E], taken[:, :], ALU.add).then_inc(aux_read, 1)
                dve.wait_ge(aux_read, u + 1)
                step(v.tensor_tensor(placed[:, :, :], place[:, :, :], chosen[:, :, :], ALU.mult))
                step(v.tensor_reduce(slot[:, :], placed[:, :, :], AX.X, ALU.add))
                step(v.tensor_tensor(keep[:, :], slot[:, :], limit[:, :], ALU.is_lt))
                step(v.scalar_tensor_tensor(kept[:, :], slot[:, :], -NOWHERE, keep[:, :], ALU.add, ALU.mult))
                v.tensor_scalar(slot_idx[g % 2][:, :], kept[:, :], NOWHERE, None, ALU.add).then_inc(slot_made, 1)

            def score(t, c):
                n, w, k = chunk_no(t, c), chunk_blocks(t, c) * P, t % 2
                lo = S - P - t % NT * P + c * GTOK
                dve.wait_ge(score_full, n + 1)
                v.tensor_tensor_reduce(sc[:, k, c * GTOK:c * GTOK + w], sc_ps[n % 2][:, 0:w], bias[:, lo:lo + w],
                                       score_mul[:, 0:1], -3e38, ALU.add, ALU.max, cmax[:, k, c:c + 1]
                                       ).then_inc(score_read, 1)
                if c == chunks(t) - 1:
                    dve.wait_ge(score_read, n + 1)
                    step(v.tensor_reduce(rmax[:, k:k + 1], cmax[:, k, 0:c + 1], AX.X, ALU.max))
                    v.tensor_scalar(nbias[:, k:k + 1], rmax[:, k:k + 1], -1.0, LN2_UP, ALU.mult, ALU.add
                                    ).then_inc(nbias_made, 1)

            def low(t, c):
                n, w = chunk_no(t, c), chunk_blocks(t, c) * P
                cols = slice(c * GTOK, c * GTOK + w)
                dve.wait_ge(pT_hi, n + 1)
                v.tensor_tensor(pT_l[:, t % 2, cols], tr_ps[n % 2][:, 0:w], pT_h[:, t % 2, cols], ALU.subtract
                                ).then_inc(pT_lo, 1)

            def finish(t):
                k, g = t % 2, t // GT
                step(v.tensor_reduce(rsum[:, k:k + 1], psums[:, t % 3, 0:chunks(t)], AX.X, ALU.add))
                step(v.reciprocal(rinv[:, k:k + 1], rsum[:, k:k + 1]))
                dve.wait_ge(pv_full, t + 1)
                if t % GT == 0 and g >= 2:
                    dve.wait_ge(rows_s[g % 2], g // 2 * 16)
                v.tensor_scalar(so[g % 2][:, t % GT, :], pv_ps[k][:, 0:D], rinv[:, k:k + 1], value_mul[:, 0:1],
                                ALU.mult, ALU.mult).then_inc(s_made, 1)

            def largest(buf, q, at=0):
                m, cols = piece(q)
                last = v.tensor_reduce(pmax[:, m, q % PIECES:q % PIECES + 1], buf[:, m, cols], AX.X, ALU.max,
                                       apply_absolute_value=True)
                if q == 2 * PIECES - 1:
                    step(last, at)
                    v.tensor_reduce(wmax[:, :], pmax[:, :, :], AX.X, ALU.max).then_inc(w_maxed, 1)

            def scale(e, k, at=0):
                dve.wait_ge(w_topped, e + 1)
                scales(wtop[:, :], wexp[:, :], wup[k][:, :], wdn[:, :], at)
                v.tensor_scalar(ymul[k][:, :], wdn[:, 0:1], wdn[:, 1:2], UNDO, ALU.mult, ALU.mult
                                ).then_inc(w_scaled, 1)

            def split_low(buf, e, k, q):
                m, cols = piece(q)
                dve.wait_ge(w_hi, e * 2 * PIECES + q + 1)
                v.scalar_tensor_tensor(w_l[k][:, m, cols], buf[:, m, cols], wup[k][:, m:m + 1], w_h[k][:, m, cols],
                                       ALU.mult, ALU.subtract).then_inc(w_lo, 1)

            def take_rows(k):
                v.tensor_scalar(pk[k][:, :], xe[:, :, PCOL], ymul[k][:, 0:1], None, ALU.mult)
                v.tensor_scalar(get_idx[k][:, :], xe[:, :, TCOL], float(T - 1), None, ALU.min)
                v.tensor_copy(put_idx[k][:, :], xe[:, :, TCOL]).then_inc(idx_made, 1)

            def turn_low(e, k, d):
                dve.wait_ge(xe_hi, e * KD + d + 1)
                v.scalar_tensor_tensor(xeT_l[k][:, d, :], aux[d][:, :], X_UP, xeT_h[k][:, d, :],
                                       ALU.mult, ALU.subtract).then_inc(xe_lo, 1)

            def hidden(m, f):
                dve.wait_ge(h_hi, m + 1)
                v.tensor_tensor(hid_l[:, f % HB, :], hid[:, f % 2, :], hid_h[:, f % HB, :], ALU.subtract
                                ).then_inc(h_lo, 1)

            beside = {VAL: query_weights, VAL + 1: lambda: norm_stats(1), VAL + 2: bias_table,
                      VAL + 3: lambda: norm_scale(1), QRY: lambda: norm_rows(1)}
            for n in range(UNITS):
                unit(0, n)
                if n in beside:
                    beside[n]()
            dve.wait_ge(masked, 1)
            score(0, 0)
            for t in range(TILES):
                for c in steps(t):
                    if c < chunks(t + 1):
                        score(t + 1, c)
                    if c < chunks(t):
                        low(t, c)
                    if c == chunks(t - 1) - 1:
                        finish(t - 1)
                    for n in units_after(t, c):
                        unit(t // GT + 1, n)
                if t % GT and t // GT + 2 < GROUPS:
                    [norm_stats, norm_scale, norm_rows][t % GT - 1](t // GT + 2)
                for q in share(FIRST_MAX, t):
                    dve.wait_ge(w_in[1], 16)
                    largest(raw, q)
                if t == FIRST_SCALE:
                    scale(0, 0)
                for q in share(FIRST_SPLIT, t):
                    split_low(raw, 0, 0, q)
                for q in share(SECOND_MAX, t):
                    dve.wait_ge(w_in[1], 32)
                    largest(raw, q)
                if t == FIRST_ROWS:
                    for d in range(KD):
                        turn_low(0, 0, d)
                    dve.wait_ge(w_scaled, 1)
                    take_rows(0)
            hidden(0, 0)
            finish(TILES - 1)
            hidden(1, 1)
            first_steps = count[0]

            def expert(i, k, more, far, at):
                e, o = i * 2 + k, 1 - k
                for f in range(NF):
                    if more or f + LEAD < NF:
                        hidden(e * NF + f + LEAD, f + LEAD)
                    if more:
                        if f == 0:
                            scale(e + 1, o, at)
                        if f in TURN_AT:
                            turn_low(e + 1, o, TURN_AT.index(f))
                        for q in SPLIT_AT.get(f, ()):
                            split_low(wraw[o], e + 1, o, q)
                        if f == NF - 2:
                            dve.wait_ge(xe_in, e * 16 + 32)
                            dve.wait_ge(w_scaled, e + 2)
                            dve.wait_ge(put_over, e + 1)
                            take_rows(o)
                    if far:
                        if f == min(MAX_AT):
                            dve.wait_ge(w_in[k], i * 16 + (48 if k else 16))
                        for q in MAX_AT.get(f, ()):
                            largest(wraw[k], q, at)

            with dve.Fori(0, E // 2 - 1) as i:
                count[0] = 0
                for k in range(2):
                    expert(i, k, True, True, i * PAIR_STEPS + first_steps)
                assert count[0] == PAIR_STEPS, count[0]
            count[0] = 0
            expert(E // 2 - 1, 0, True, False, (E // 2 - 1) * PAIR_STEPS + first_steps)
            expert(E // 2 - 1, 1, False, False, 0)
            for j in range(SJ):
                dve.wait_ge(gate_made, (E - 1) * SJ + j + 1 + 2 * SJ)
                dve.wait_ge(back_in[j], E * 16)
                v.tensor_tensor(gate[:, j, :], gate[:, j, :], back[j][:, D:2 * D], ALU.mult).then_inc(gated, 1)
                dve.wait_ge(gated, (E - 1) * SJ + j + 1)
                v.tensor_tensor(back[j][:, 0:D], gate[:, j, :], back[j][:, 0:D], ALU.add).then_inc(done_made, 1)

        @block.scalar
        def _(act):
            a_ = nc.scalar
            act.dma_start(xg[0][:, :, :], x_g[0]).then_inc(x_in[0], 16)

            def unit(g, n):
                if n == RANK:
                    return
                u = g * UNITS + n
                a, at = aux[u % 2], key_slot(g // NG, g % NG)
                act.wait_ge(aux_full, u + 1)
                if n < VAL:
                    a_.activation(xT_h[:, n, at, :], a[:, :], ACT.Copy, scale=X_UP).then_inc(hi_made, 1)
                elif n < QRY:
                    a_.activation(v_h[:, at, n - VAL, :], a[:, 0:D], ACT.Copy, scale=ACC_DOWN).then_inc(hi_made, 1)
                    if n == QRY - 1:
                        act.wait_ge(below_made, g + 1)
                        a_.activation(lexp[:, :, :], below[:, :, :], ACT.Exp).then_inc(lexp_made, 1)
                else:
                    a_.activation(qT_h[g % 2][:, n - QRY, :], a[:, :], ACT.Copy, scale=ACC_DOWN).then_inc(hi_made, 1)

            def probs(t):
                k = t % 2
                act.wait_ge(nbias_made, t + 1)
                for c in range(chunks(t)):
                    cols = slice(c * GTOK, c * GTOK + chunk_blocks(t, c) * P)
                    a_.activation(sc[:, k, cols], sc[:, k, cols], ACT.Exp, bias=nbias[:, k:k + 1],
                                  accum_out=psums[:, t % 3, c:c + 1]).then_inc(exp_made, 1)

            def high(t, c):
                n, w = chunk_no(t, c), chunk_blocks(t, c) * P
                act.wait_ge(turned, n + 1)
                a_.activation(pT_h[:, t % 2, c * GTOK:c * GTOK + w], tr_ps[n % 2][:, 0:w], ACT.Copy
                              ).then_inc(pT_hi, 1)

            def split_high(buf, e, k, q):
                m, cols = piece(q)
                act.wait_ge(w_scaled, e + 1)
                a_.activation(w_h[k][:, m, cols], buf[:, m, cols], ACT.Copy, scale=wup[k][:, m:m + 1]
                              ).then_inc(w_hi, 1)

            def turn_high(e, k, d):
                act.wait_ge(xe_turned, e * KD + d + 1)
                a_.activation(xeT_h[k][:, d, :], aux[d][:, :], ACT.Copy, scale=X_UP).then_inc(xe_hi, 1)

            def hidden(m, f, first=False):
                act.wait_ge(h_full, m + 1)
                if not first:
                    act.wait_ge(h_lo, m - 1)
                a_.activation(hid[:, f % 2, :], sc_ps[f % 2][:, :], ACT.Relu, scale=ACC_DOWN).then_inc(h_read, 1)
                act.wait_ge(h_read, m + 1)
                a_.activation(hid_h[:, f % HB, :], hid[:, f % 2, :], ACT.Copy).then_inc(h_hi, 1)

            act.wait_ge(small_scaled, 1)
            a_.activation(wvr_h[:, :, D:D + E], wsmall[:, 2, :, 0:E], ACT.Copy, scale=small_up[:, 2:3]
                          ).then_inc(small_hi, 1)
            for k in range(KD):
                act.wait_ge(wv_turned, k + 1)
                a_.activation(wvr_h[:, k, 0:D], tr_ps[k][:, 0:D], ACT.Copy, scale=small_up[:, 1:2]
                              ).then_inc(small_hi, 1)
            a_.activation(wqk_h[:, :, :], wsmall[:, 0], ACT.Copy, scale=small_up[:, 0:1]).then_inc(small_hi, 1)
            for n in range(UNITS):
                unit(0, n)
            probs(0)
            for t in range(TILES):
                for c in steps(t):
                    if c < chunks(t):
                        high(t, c)
                    if c == chunks(t) - 1 and c < chunks(t + 1) and last_step(t, c):
                        probs(t + 1)
                    for n in units_after(t, c):
                        unit(t // GT + 1, n)
                if t + 1 < TILES and not (len(steps(t)) == chunks(t) <= chunks(t + 1)):
                    probs(t + 1)
                for q in share(FIRST_SPLIT, t):
                    split_high(raw, 0, 0, q)
                if t == FIRST_ROWS:
                    for d in range(KD):
                        turn_high(0, 0, d)
            act.wait_ge(consts_made, 1)
            a_.activation(warm[:, :], empty[:, 0:1], ACT.Silu)
            for f in range(LEAD):
                hidden(f, f, True)

            def expert(i, k, more):
                e, o = i * 2 + k, 1 - k
                for f in range(NF):
                    if more or f + LEAD < NF:
                        hidden(e * NF + f + LEAD, f + LEAD)
                    if more:
                        if f in TURN_AT:
                            turn_high(e + 1, o, TURN_AT.index(f))
                        for q in SPLIT_AT.get(f, ()):
                            split_high(wraw[o], e + 1, o, q)
                act.wait_ge(idx_made, e + 1)
                for j in range(SJ):
                    act.wait_ge(y_full, e * (SJ // 2) + j // 2 + 1)
                    act.wait_ge(done_made, e * SJ + SJ)
                    a_.activation(gate[:, j, :], y_ps[k][j], ACT.Silu, scale=pk[k][:, j:j + 1]).then_inc(gate_made, 1)

            with act.Fori(0, E // 2 - 1) as i:
                for k in range(2):
                    expert(i, k, True)
            expert(E // 2 - 1, 0, True)
            expert(E // 2 - 1, 1, False)

        @block.tensor
        def _(pe):
            def product(ps, a_h, a_l, b_h, b_l, first, last, shared=False):
                pe.matmul(ps, a_h, b_h, start=first, stop=False, skip_group_check=shared)
                pe.matmul(ps, a_h, b_l, start=False, stop=False, skip_group_check=shared)
                return pe.matmul(ps, a_l, b_h, start=False, stop=last, skip_group_check=shared)

            def unit(g, n):
                u = g * UNITS + n
                a, at = aux[u % 2], key_slot(g // NG, g % NG)
                if u >= 2:
                    pe.wait_ge(aux_read, u - 1)
                if n < VAL:
                    if n == 0:
                        pe.wait_ge(xn_made, g + 1)
                    for j in range(GT):
                        last = pe.transpose(a[:, j * P:(j + 1) * P], xnr[g % 2][:, j, n * P:(n + 1) * P], ident[:, :])
                elif n < QRY:
                    if n == VAL:
                        pe.wait_ge(aux_read, u)
                        if g == 0:
                            pe.wait_ge(values_ready, 1)
                    rows_ = slice((n - VAL) * P, (n - VAL + 1) * P)
                    for d in range(KD):
                        last = product(a[:, 0:D + E], xT_h[:, d, at, rows_], xT_l[:, d, at, rows_],
                                       wvr_h[:, d, :], wvr_l[:, d, :], d == 0, d == KD - 1)
                elif n < RANK:
                    cols = slice((n - QRY) * P, (n - QRY + 1) * P)
                    if u == QRY:
                        pe.wait_ge(ready, 1)
                    for d in range(KD):
                        last = product(a[:, :], wqk_h[:, d, cols], wqk_l[:, d, cols],
                                       xT_h[:, d, at, :], xT_l[:, d, at, :], d == 0, d == KD - 1)
                else:
                    pe.wait_ge(chosen_made, g + 1)
                    pe.matmul(a[:, 0:GT * E], before[:, :], chosen[:, :, :], start=True, stop=False,
                              skip_group_check=True)
                    for j in range(GT - 1):
                        pe.matmul(a[:, (j + 1) * E:GT * E], ones[:, :],
                                  chosen[:, j:j + 1, :].to_broadcast([P, GT - 1 - j, E]),
                                  start=False, stop=False, skip_group_check=True)
                    for j in range(GT):
                        last = pe.matmul(a[:, GT * E:GT * E + E], ones[:, :], chosen[:, j, :], start=False,
                                         stop=j == GT - 1, skip_group_check=True)
                last.then_inc(aux_full, 1)

            def score(t, c):
                n, w, g = chunk_no(t, c), chunk_blocks(t, c) * P, t // GT
                at = key_slot(t // NT, c)
                if c == 0 and t % GT == 0:
                    pe.wait_ge(aux_read, g * UNITS + HALVED)
                if n >= 2:
                    pe.wait_ge(score_read, n - 1)
                rows_ = slice(t % GT * P, (t % GT + 1) * P)
                for d in range(KD):
                    last = product(sc_ps[n % 2][:, 0:w], qT_h[g % 2][:, d, rows_], qT_l[g % 2][:, d, rows_],
                                   xT_h[:, d, at, 0:w], xT_l[:, d, at, 0:w], d == 0, d == KD - 1)
                last.then_inc(score_full, 1)

            def turn(t, c):
                n = chunk_no(t, c)
                pe.wait_ge(exp_made, n + 1)
                if n >= 2:
                    pe.wait_ge(pT_lo, n - 1)
                for q in range(chunk_blocks(t, c)):
                    col = c * GTOK + q * P
                    last = pe.transpose(tr_ps[n % 2][:, q * P:(q + 1) * P], sc[:, t % 2, col:col + P], ident[:, :])
                last.then_inc(turned, 1)

            def values(t, c):
                n, at = chunk_no(t, c), key_slot(t // NT, c)
                pe.wait_ge(pT_lo, n + 1)
                if c == 0 and t >= 2:
                    pe.wait_ge(s_made, t - 1)
                for q in range(chunk_blocks(t, c)):
                    kb = c * GT + q
                    rows_ = slice(kb * P, (kb + 1) * P)
                    last = product(pv_ps[t % 2][:, 0:D], pT_h[:, t % 2, rows_], pT_l[:, t % 2, rows_],
                                   v_h[:, at, q, :], v_l[:, at, q, :], kb == 0, kb == t % NT)
                if c == chunks(t) - 1:
                    last.then_inc(pv_full, 1)

            def turn_rows(e, d):
                if d == 0:
                    pe.wait_ge(xe_in, e * 16 + 16)
                for j in range(SJ):
                    last = pe.transpose(aux[d][:, j * P:(j + 1) * P], xe[:, j, d * P:(d + 1) * P], ident[:, :])
                last.then_inc(xe_turned, 1)

            def up(e, f, k, first=False):
                if f == 0:
                    pe.wait_ge(w_lo, e * 2 * PIECES + PIECES)
                    pe.wait_ge(xe_lo, e * KD + KD)
                if not first:
                    pe.wait_ge(h_read, e * NF + f - 1)
                for d in range(KD):
                    cols = slice(d * F + f * P, d * F + (f + 1) * P)
                    last = product(sc_ps[f % 2][:, :], w_h[k][:, 0, cols], w_l[k][:, 0, cols],
                                   xeT_h[k][:, d, :], xeT_l[k][:, d, :], d == 0, d == KD - 1)
                last.then_inc(h_full, 1)

            def down(e, f, k):
                if f == 0:
                    pe.wait_ge(w_lo, (e + 1) * 2 * PIECES)
                    pe.wait_ge(gate_made, (e + 1) * SJ)
                pe.wait_ge(h_lo, e * NF + f + 1)
                cols = slice(f * D, (f + 1) * D)
                for j in range(SJ):
                    rows_ = slice(j * P, (j + 1) * P)
                    last = product(y_ps[k][j], hid_h[:, f % HB, rows_], hid_l[:, f % HB, rows_],
                                   w_h[k][:, 1, cols], w_l[k][:, 1, cols], f == 0 and j % 2 == 0, f == NF - 1, True)
                    if f == NF - 1 and j % 2:
                        last.then_inc(y_full, 1)

            pe.wait_ge(small_in, 64)
            pe.wait_ge(consts_made, 8)
            for k in range(KD):
                for j in range(KD):
                    last = pe.transpose(tr_ps[k][:, j * P:(j + 1) * P], wsmall[:, 1, j, k * P:(k + 1) * P], ident[:, :])
                last.then_inc(wv_turned, 1)
            for n in range(UNITS):
                unit(0, n)
            score(0, 0)
            for t in range(TILES):
                for c in steps(t):
                    if c < chunks(t + 1):
                        score(t + 1, c)
                    if c < chunks(t - 1):
                        values(t - 1, c)
                    if c < chunks(t):
                        turn(t, c)
                    for n in units_after(t, c):
                        unit(t // GT + 1, n)
                if t == FIRST_ROWS:
                    pe.wait_ge(aux_read, GROUPS * UNITS)
                    for d in range(KD):
                        turn_rows(0, d)
            pe.wait_ge(score_read, ALL_CHUNKS)
            up(0, 0, 0, True)
            for c in range(chunks(TILES - 1)):
                values(TILES - 1, c)
            up(0, 1, 0, True)
            pe.wait_ge(s_made, TILES)

            def expert(i, k, more):
                e, o = i * 2 + k, 1 - k
                for f in range(NF):
                    if f + LEAD < NF:
                        up(e, f + LEAD, k)
                    elif more:
                        up(e + 1, f + LEAD - NF, o)
                    if more and f in TURN_AT:
                        d = TURN_AT.index(f)
                        pe.wait_ge(xe_lo, e * KD + d + 1)
                        turn_rows(e + 1, d)
                    down(e, f, k)

            with pe.Fori(0, E // 2 - 1) as i:
                for k in range(2):
                    expert(i, k, True)
            expert(E // 2 - 1, 0, True)
            expert(E // 2 - 1, 1, False)


_INS = ["L0_attn_x", "L0_attn_W_qk", "L0_attn_W_v", "L0_attn_alibi_slope", "L0_ffn_Wr"]


def kernel(**inputs):
    import numpy as np
    import concourse.bacc as bacc
    from concourse.bass_utils import run_bass_kernel_spmd

    def plain(name):
        return np.ascontiguousarray(np.asarray(inputs[name]))

    w1 = plain("L0_ffn_W1").reshape(E, KD, P, F).transpose(0, 2, 1, 3).reshape(E, P, WCOLS)
    w2 = plain("L0_ffn_W2").reshape(E, NF, P, D).transpose(0, 2, 1, 3).reshape(E, P, WCOLS)
    arrays = {
        "in_x": plain("L0_attn_x").reshape(T, D), "in_w_qk": plain("L0_attn_W_qk"), "in_w_v": plain("L0_attn_W_v"),
        "in_slope": plain("L0_attn_alibi_slope"), "in_w_r": plain("L0_ffn_Wr"),
        "in_w_e": np.ascontiguousarray(np.stack([w1, w2], axis=1)),
    }
    nc = bacc.Bacc("TRN2", target_bir_lowering=False, num_devices=1)
    args = [nc.dram_tensor(n, a.shape, mybir.dt.from_np(a.dtype), kind="ExternalInput").ap()
            for n, a in arrays.items()]
    args.append(nc.dram_tensor("out_0", (T, D), F32, kind="ExternalOutput").ap())
    args.append(nc.dram_tensor("slots", (T, ROW), F32).ap())
    args.append(nc.dram_tensor("rows", (T, 2 * D), F32).ap())
    layer_kernel(nc, *args)
    r = run_bass_kernel_spmd(nc, [arrays], core_ids=[0])
    return r.results[0]["out_0"].reshape(B, S, D)
```

```python
from contextlib import ExitStack

import concourse.bass as bass
from concourse import mybir

P = 128
B, S, D = 2, 2048, 256
E, F = 8, 1024
T = B * S
CAP = T // E
KD = D // P
NT = S // P
TILES = B * NT
GT = 4
GTOK = GT * P
NG = NT // GT
GROUPS = B * NG
NF = F // P
SJ = CAP // P
ROW = D + 8
PCOL, TCOL = D, D + 1
NOWHERE = float(1 << 20)
PIECE = 512
WCOLS = KD * F
PIECES = WCOLS // PIECE

X_UP = 2.0 ** 10
ACC_DOWN = 2.0 ** -18
W_TOP = 14
UNDO = 2.0 ** 8
SM_SCALE = 2.0 ** -4
LN2_UP = 14 * 0.6931471805599453
EPS = 1e-5

HALVED = 8
XT, QRY, VAL = 0, KD, 2 * KD
RANK = HALVED
UNITS = HALVED + 1
PAIR_STEPS = 2 * 5
HB = 4
LEAD = 2
TURN_AT = (1, 3)
SPLIT_AT = {1: (0,), 2: (1, 2), 3: (3,), 4: (4, 5), 5: (6, 7)}
MAX_AT = {5: (0,), 6: (1, 2, 3), 7: (4, 5, 6, 7)}

F32 = mybir.dt.float32
F16 = mybir.dt.float16
I32 = mybir.dt.int32
U32 = mybir.dt.uint32
ALU = mybir.AluOpType
ACT = mybir.ActivationFunctionType
AX = mybir.AxisListType
RMAX = bass.bass_isa.ReduceOp.absmax


def chunks(t):
    return t % NT // GT + 1 if 0 <= t < TILES else 0


def chunk_no(t, c):
    return sum(chunks(k) for k in range(t)) + c


def chunk_blocks(t, c):
    return GT if c < chunks(t) - 1 else t % GT + 1


def key_slot(b, g):
    return g if g else b * NG


ALL_CHUNKS = sum(chunks(t) for t in range(TILES))


def layer_kernel(nc, x, w_qk, w_v, slope, w_r, w_e, out, slots, rows):
    with ExitStack() as ctx:
        def sb(name, shape, dt=F32):
            return ctx.enter_context(nc.sbuf_tensor(name, shape, dt))

        def sem(name):
            return ctx.enter_context(nc.semaphore(name))

        ident = sb("ident", [P, P])
        before = sb("before", [P, P], F16)
        ones = sb("ones", [P, P], F16)
        ranks = sb("ranks", [P, GT, E])
        bias = sb("bias", [P, S])
        slope_c = sb("slope_c", [P, 1])
        wqk_h = sb("wqk_h", [P, KD, D], F16)
        wqk_l = sb("wqk_l", [P, KD, D], F16)
        wvr_h = sb("wvr_h", [P, KD, D + E], F16)
        wvr_l = sb("wvr_l", [P, KD, D + E], F16)
        small_max = sb("small_max", [P, 3])
        small_top = sb("small_top", [P, 3])
        small_exp = sb("small_exp", [P, 3])
        small_up = sb("small_up", [P, 3])
        small_dn = sb("small_dn", [P, 3])
        score_mul = sb("score_mul", [P, 1])
        bias_mul = sb("bias_mul", [P, 1])
        value_mul = sb("value_mul", [P, 1])
        logit_mul = sb("logit_mul", [P, 1])
        empty = sb("empty", [P, ROW])

        xg = [sb(f"xg{k}", [P, GT, D]) for k in range(2)]
        so = [sb(f"so{k}", [P, GT, D]) for k in range(2)]
        xnr = [sb(f"xnr{k}", [P, GT, ROW]) for k in range(2)]
        stats = sb("stats", [P, GT, 6])
        mv = sb("mv", [P, GT, 2])
        var = sb("var", [P, GT])
        power = sb("power", [P, GT])
        rec = sb("rec", [P, GT])
        sq = sb("sq", [P, GT])
        sqv = sb("sqv", [P, GT])
        newton = sb("newton", [P, GT])
        rstd = sb("rstd", [P, GT])
        xT_h = sb("xT_h", [P, KD, NG + 1, GTOK], F16)
        xT_l = sb("xT_l", [P, KD, NG + 1, GTOK], F16)
        v_h = sb("v_h", [P, NG + 1, GT, D], F16)
        v_l = sb("v_l", [P, NG + 1, GT, D], F16)
        qT_h = [sb(f"qT_h{k}", [P, KD, GTOK], F16) for k in range(2)]
        qT_l = [sb(f"qT_l{k}", [P, KD, GTOK], F16) for k in range(2)]
        logits = sb("logits", [P, GT, E])
        lmax = sb("lmax", [P, GT])
        below = sb("below", [P, GT, E])
        lexp = sb("lexp", [P, GT, E])
        lsum = sb("lsum", [P, GT])
        key = sb("key", [P, GT, E])
        kmax = sb("kmax", [P, GT])
        chosen = sb("chosen", [P, GT, E], F16)
        counts = sb("counts", [P, GT + 1, E])
        place = sb("place", [P, GT, E])
        placed = sb("placed", [P, GT, E])
        sum4 = sb("sum4", [P, GT, E // 2])
        sum2 = sb("sum2", [P, GT, E // 4])
        slot = sb("slot", [P, GT])
        room = sb("room", [P, GT])
        far = sb("far", [P, GT])
        limit = sb("limit", [P, GT])
        keep = sb("keep", [P, GT])
        kept = sb("kept", [P, GT])
        slot_idx = [sb(f"slot_idx{k}", [P, GT], U32) for k in range(2)]
        taken = sb("taken", [P, E])
        token = sb("token", [P, GT])

        sc = sb("sc", [P, 2, S])
        cmax = sb("cmax", [P, 2, NG])
        rmax = sb("rmax", [P, 2])
        nbias = sb("nbias", [P, 2])
        psums = sb("psums", [P, 3, NG])
        rsum = sb("rsum", [P, 2])
        rinv = sb("rinv", [P, 2])
        pT_h = sb("pT_h", [P, 2, S], F16)
        pT_l = sb("pT_l", [P, 2, S], F16)
        wsmall = sc[:, 1, 0:3 * KD * D].rearrange("p (a k n) -> p a k n", a=3, k=KD)

        raw = sb("raw", [P, 2, WCOLS])
        wraw = [sc, raw]
        w_h = [sb(f"w_h{k}", [P, 2, WCOLS], F16) for k in range(2)]
        w_l = [sb(f"w_l{k}", [P, 2, WCOLS], F16) for k in range(2)]
        pmax = sb("pmax", [P, 2, PIECES])
        wmax = sb("wmax", [P, 2])
        wtop = sb("wtop", [P, 2])
        wexp = sb("wexp", [P, 2])
        wup = [sb(f"wup{k}", [P, 2]) for k in range(2)]
        wdn = sb("wdn", [P, 2])
        ymul = [sb(f"ymul{k}", [P, 1]) for k in range(2)]
        xe = sb("xe", [P, SJ, ROW])
        xeT_h = [sb(f"xeT_h{k}", [P, KD, CAP], F16) for k in range(2)]
        xeT_l = [sb(f"xeT_l{k}", [P, KD, CAP], F16) for k in range(2)]
        pk = [sb(f"pk{k}", [P, SJ]) for k in range(2)]
        get_idx = [sb(f"get_idx{k}", [P, SJ], U32) for k in range(2)]
        put_idx = [sb(f"put_idx{k}", [P, SJ], U32) for k in range(2)]
        hid = sb("hid", [P, 2, CAP])
        hid_h = sb("hid_h", [P, HB, CAP], F16)
        hid_l = sb("hid_l", [P, HB, CAP], F16)
        gate = sb("gate", [P, SJ, D])
        back = [sb(f"back{j}", [P, 2 * D]) for j in range(SJ)]
        warm = sb("warm", [P, 1])

        bank = [ctx.enter_context(nc.psum_tensor(f"bank{k}", [P, 512], F32)) for k in range(8)]
        sc_ps, tr_ps, pv_ps, aux = bank[0:2], bank[2:4], bank[4:6], bank[6:8]
        y_ps = [[bank[2 + 2 * k + j // 2][:, j % 2 * D:(j % 2 + 1) * D] for j in range(SJ)] for k in range(2)]

        x_in = [sem(f"x_in{k}") for k in range(2)]
        small_in = sem("small_in")
        slots_empty = sem("slots_empty")
        out_first = [sem(f"out_first{k}") for k in range(2)]
        rows_x = [sem(f"rows_x{k}") for k in range(2)]
        rows_s = [sem(f"rows_s{k}") for k in range(2)]
        slots_out = [sem(f"slots_out{k}") for k in range(2)]
        w_in = [sem("w_in_sc"), sem("w_in_raw")]
        xe_in = sem("xe_in")
        back_in = [sem(f"back_in{j}") for j in range(SJ)]
        out_put = [sem(f"out_put{j}") for j in range(SJ)]
        consts_made = sem("consts_made")
        small_maxed = sem("small_maxed")
        small_topped = sem("small_topped")
        wv_turned = sem("wv_turned")
        bias_made = sem("bias_made")
        masked = sem("masked")
        small_scaled = sem("small_scaled")
        small_hi = sem("small_hi")
        values_ready = sem("values_ready")
        ready = sem("ready")
        bias_raw = sem("bias_raw")
        pool_step = sem("pool_step")
        dve_step = sem("dve_step")
        var_made = sem("var_made")
        rstd_made = sem("rstd_made")
        xn_made = sem("xn_made")
        aux_full = sem("aux_full")
        aux_read = sem("aux_read")
        hi_made = sem("hi_made")
        below_made = sem("below_made")
        lexp_made = sem("lexp_made")
        chosen_made = sem("chosen_made")
        prob_set = sem("prob_set")
        slot_made = sem("slot_made")
        score_full = sem("score_full")
        score_read = sem("score_read")
        nbias_made = sem("nbias_made")
        exp_made = sem("exp_made")
        turned = sem("turned")
        pT_hi = sem("pT_hi")
        pT_lo = sem("pT_lo")
        pv_full = sem("pv_full")
        s_made = sem("s_made")
        w_maxed = sem("w_maxed")
        w_topped = sem("w_topped")
        w_scaled = sem("w_scaled")
        w_hi = sem("w_hi")
        w_lo = sem("w_lo")
        xe_turned = sem("xe_turned")
        xe_hi = sem("xe_hi")
        xe_lo = sem("xe_lo")
        idx_made = sem("idx_made")
        h_full = sem("h_full")
        h_read = sem("h_read")
        h_hi = sem("h_hi")
        h_lo = sem("h_lo")
        y_full = sem("y_full")
        gate_made = sem("gate_made")
        gated = sem("gated")
        done_made = sem("done_made")
        put_over = sem("put_over")
        passed = sem("passed")

        x_g = x.rearrange("(g j p) d -> g p j d", p=P, j=GT)
        out_g = out.rearrange("(g j p) d -> g p j d", p=P, j=GT)
        rows_g = rows.rearrange("(g j p) d -> g p j d", p=P, j=GT)
        slots_e = slots.rearrange("(e j p) d -> e p j d", p=P, j=SJ)
        w_k = w_e.rearrange("e k p n -> e p k n")

        block = ctx.enter_context(nc.Block())

        def steps(t):
            return range(max(chunks(t + 1), chunks(t), chunks(t - 1)))

        def last_step(t, c):
            return c == len(steps(t)) - 1

        def units_after(t, c):
            g, j = t // GT + 1, t % GT
            first, last = c == 0, last_step(t, c)
            late = [(0, RANK)] * (t == 0 and first)
            if g == GROUPS:
                return late
            if j == 0:
                mine = [XT, XT + 1] * first + [QRY, QRY + 1] * last
            else:
                mine = [[VAL, VAL + 1], [VAL + 2, VAL + 3], [RANK]][j - 1] * first
            return late + [(g, n) for n in mine]

        FIRST_MAX, FIRST_SCALE, FIRST_SPLIT = (4, 5, 6, 7), 8, tuple(range(8, 16))
        SECOND_MAX = (22, 23, 24, 25, 26, 27, 28, 29)
        FIRST_ROWS = TILES - 2

        def share(tiles, t):
            n = 2 * PIECES // len(tiles)
            return range(tiles.index(t) * n, (tiles.index(t) + 1) * n) if t in tiles else ()

        def piece(q):
            return q // PIECES, slice(q % PIECES * PIECE, (q % PIECES + 1) * PIECE)

        def apart(eng):
            eng.sem_inc(passed, 1)

        @block.sync
        def _(sp):
            sp.dma_start(wsmall[:, 0], w_qk.rearrange("(k p) n -> p k n", p=P)).then_inc(small_in, 16)
            sp.dma_start(wsmall[:, 1], w_v.rearrange("(k p) n -> p k n", p=P)).then_inc(small_in, 16)
            sp.dma_start(wsmall[:, 2, :, 0:E], w_r.rearrange("(k p) n -> p k n", p=P)).then_inc(small_in, 16)
            sp.dma_start(slope_c[:, :], slope.rearrange("(o n) -> o n", o=1).partition_broadcast(P)
                         ).then_inc(small_in, 16)
            sp.wait_ge(small_in, 64)
            sp.wait_ge(x_in[0], 16)
            sp.dma_start(xg[1][:, :, :], x_g[1]).then_inc(x_in[1], 16)
            sp.wait_ge(consts_made, 1)
            sp.dma_start(slots.rearrange("(k p) r -> p k r", p=P),
                         empty[:, :].unsqueeze(1).to_broadcast([P, T // P, ROW])).then_inc(slots_empty, 16)
            sp.dma_start(raw[:, :, :], w_k[0]).then_inc(w_in[1], 16)
            for g in range(GROUPS):
                k, n = g % 2, (g // 2 + 1) * 16
                sp.wait_ge(x_in[k], n)
                sp.dma_start(out_g[g], xg[k][:, :, :]).then_inc(out_first[k], 16)
                sp.dma_start(rows_g[g][:, :, 0:D], xg[k][:, :, :]).then_inc(rows_x[k], 16)
                if g + 2 < GROUPS:
                    sp.wait_ge(xn_made, g + 1)
                    sp.wait_ge(out_first[k], n)
                    sp.wait_ge(rows_x[k], n)
                    sp.dma_start(xg[k][:, :, :], x_g[g + 2]).then_inc(x_in[k], 16)
                if g > 0:
                    sp.wait_ge(s_made, g * GT)
                    sp.dma_start(rows_g[g - 1][:, :, D:2 * D], so[1 - k][:, :, :]).then_inc(rows_s[1 - k], 16)
                if g == NG:
                    sp.wait_ge(w_lo, 2 * PIECES)
                    sp.dma_start(raw[:, :, :], w_k[1]).then_inc(w_in[1], 16)
            for k in range(2):
                sp.wait_ge(slots_out[k], GROUPS // 2 * GT * 16)
            sp.dma_start(xe[:, :, :], slots_e[0]).then_inc(xe_in, 16)
            sp.wait_ge(turned, ALL_CHUNKS)
            sp.dma_start(sc[:, :, :], w_k[2]).then_inc(w_in[0], 16)
            sp.wait_ge(s_made, TILES)
            sp.dma_start(rows_g[GROUPS - 1][:, :, D:2 * D], so[1][:, :, :]).then_inc(rows_s[1], 16)

            def next_rows(e):
                sp.wait_ge(xe_turned, e * KD)
                sp.wait_ge(idx_made, e)
                sp.dma_start(xe[:, :, :], slots_e[e] if isinstance(e, int) else slots_e[bass.ds(e, 1)]
                             ).then_inc(xe_in, 16)

            def next_weights(e, k):
                sp.wait_ge(w_lo, (e - 1) * 2 * PIECES)
                sp.dma_start(wraw[k][:, :, :], w_k[e] if isinstance(e, int) else w_k[bass.ds(e, 1)]
                             ).then_inc(w_in[k], 16)

            next_rows(1)
            with sp.Fori(0, (E - 4) // 2) as i:
                for k in range(2):
                    next_rows(i * 2 + k + 2)
                    next_weights(i * 2 + k + 3, 1 - k)
            next_rows(E - 2)
            next_weights(E - 1, 1)
            next_rows(E - 1)

        @block.gpsimd
        def _(pool):
            g_ = nc.gpsimd
            count = [0]

            def step(ins):
                count[0] += 1
                ins.then_inc(pool_step, 1)

            def settle():
                pool.wait_ge(pool_step, count[0])

            step(g_.memset(empty[:, :], 0.0))
            settle()
            g_.memset(empty[:, TCOL:TCOL + 1], NOWHERE).then_inc(consts_made, 1)
            step(g_.memset(ident[:, :], 0.0))
            step(g_.memset(ones[:, :], 1.0))
            step(g_.memset(power[:, :], -0.5))
            settle()
            g_.affine_select(out=ident[:, :], in_=ident[:, :], compare_op=ALU.not_equal, fill=1.0, base=0,
                             pattern=[[-1, P]], channel_multiplier=1).then_inc(consts_made, 1)
            g_.affine_select(out=before[:, :], in_=ones[:, :], compare_op=ALU.is_gt, fill=0.0, base=0,
                             pattern=[[1, P]], channel_multiplier=-1).then_inc(consts_made, 1)
            g_.iota(ranks[:, :, :], pattern=[[0, GT], [-1, E]], base=E, channel_multiplier=0,
                    allow_small_or_imprecise_dtypes=True).then_inc(consts_made, 1)
            g_.iota(taken[:, :], pattern=[[CAP, E]], base=0, channel_multiplier=0,
                    allow_small_or_imprecise_dtypes=True).then_inc(consts_made, 1)
            g_.iota(token[:, :], pattern=[[P, GT]], base=0, channel_multiplier=1,
                    allow_small_or_imprecise_dtypes=True).then_inc(consts_made, 1)
            for k in range(2):
                g_.memset(xnr[k][:, :, D:ROW], 0.0).then_inc(consts_made, 1)
            g_.iota(bias[:, :], pattern=[[1, S]], base=P - S, channel_multiplier=-1,
                    allow_small_or_imprecise_dtypes=True).then_inc(bias_raw, 1)

            def inverse(g):
                pool.wait_ge(var_made, g + 1)
                step(g_.tensor_tensor(rec[:, :], var[:, :], power[:, :], ALU.pow))
                settle()
                step(g_.tensor_tensor(sq[:, :], rec[:, :], rec[:, :], ALU.mult))
                settle()
                step(g_.tensor_tensor(sqv[:, :], sq[:, :], var[:, :], ALU.mult))
                settle()
                step(g_.tensor_scalar(newton[:, :], sqv[:, :], -0.5, 1.5, ALU.mult, ALU.add))
                settle()
                g_.tensor_tensor(rstd[:, :], newton[:, :], rec[:, :], ALU.mult).then_inc(rstd_made, 1)

            def normed(g):
                pool.wait_ge(rstd_made, g + 1)
                pool.wait_ge(slots_out[g % 2], g // 2 * GT * 16)
                for j in range(GT):
                    last = g_.tensor_scalar(xnr[g % 2][:, j, 0:D], xg[g % 2][:, j, :], mv[:, j, 0:1],
                                            rstd[:, j:j + 1], ALU.subtract, ALU.mult)
                last.then_inc(xn_made, 1)

            def route(g):
                pool.wait_ge(aux_read, (g + 1) * UNITS)
                step(g_.tensor_tensor(place[:, :, :], counts[:, 0:GT, :],
                                      taken[:, :].unsqueeze(1).to_broadcast([P, GT, E]), ALU.add))
                settle()
                step(g_.tensor_tensor(taken[:, :], counts[:, GT, :], taken[:, :], ALU.add))
                step(g_.tensor_tensor(placed[:, :, :], place[:, :, :], chosen[:, :, :], ALU.mult))
                settle()
                step(g_.tensor_tensor(sum4[:, :, :], placed[:, :, 0:4], placed[:, :, 4:8], ALU.add))
                settle()
                step(g_.tensor_tensor(sum2[:, :, :], sum4[:, :, 0:2], sum4[:, :, 2:4], ALU.add))
                settle()
                step(g_.tensor_tensor(slot[:, :], sum2[:, :, 0], sum2[:, :, 1], ALU.add))
                settle()
                step(g_.tensor_scalar(far[:, :], slot[:, :], -NOWHERE, None, ALU.add))
                step(g_.tensor_tensor(room[:, :], slot[:, :], limit[:, :], ALU.subtract))
                settle()
                step(g_.tensor_scalar(keep[:, :], room[:, :], 0.0, None, ALU.is_lt))
                settle()
                step(g_.tensor_tensor(kept[:, :], far[:, :], keep[:, :], ALU.mult))
                settle()
                g_.tensor_scalar(slot_idx[g % 2][:, :], kept[:, :], NOWHERE, None, ALU.add).then_inc(slot_made, 1)

            inverse(0)
            pool.wait_ge(small_maxed, 1)
            g_.partition_all_reduce(small_top[:, :], small_max[:, :], P, RMAX).then_inc(small_topped, 1)
            pool.wait_ge(bias_made, 1)
            g_.affine_select(out=bias[:, S - P:S], in_=bias[:, S - P:S], compare_op=ALU.is_ge, fill=-3e38,
                             base=0, pattern=[[-1, P]], channel_multiplier=1).then_inc(masked, 1)
            pool.sem_inc(gate_made, 2 * SJ)
            pool.sem_inc(done_made, SJ)
            pool.sem_inc(put_over, 1)
            pool.wait_ge(slots_empty, 16)

            def top(e):
                pool.wait_ge(w_maxed, e + 1)
                apart(pool)
                g_.partition_all_reduce(wtop[:, :], wmax[:, :], P, RMAX).then_inc(w_topped, 1)

            for g in range(GROUPS):
                k = g % 2
                if g + 1 < GROUPS:
                    inverse(g + 1)
                    if g + 1 >= 2:
                        normed(g + 1)
                pool.wait_ge(xn_made, g + 1)
                step(g_.tensor_copy(xnr[k][:, :, TCOL], token[:, :]))
                settle()
                step(g_.tensor_scalar(token[:, :], token[:, :], float(GTOK), None, ALU.add))
                route(g)
                pool.wait_ge(prob_set, g + 1)
                pool.wait_ge(slot_made, g + 1)
                for j in range(GT):
                    g_.indirect_dma_start(
                        slots[:, :], bass.IndirectOffsetOnAxis(ap=slot_idx[k][:, j:j + 1], axis=0),
                        xnr[k][:, j, :], None, bounds_check=T - 1, oob_is_err=False).then_inc(slots_out[k], 16)
                if g == FIRST_MAX[0] // GT + 1:
                    top(0)
            top(1)

            def fetch(e, k, j):
                g_.indirect_dma_start(
                    back[j][:, :], None, rows[:, :],
                    bass.IndirectOffsetOnAxis(ap=get_idx[k][:, j:j + 1], axis=0)).then_inc(back_in[j], 16)

            for k in range(2):
                pool.wait_ge(rows_s[k], GROUPS // 2 * 16)
                pool.wait_ge(rows_x[k], GROUPS // 2 * 16)
                pool.wait_ge(out_first[k], GROUPS // 2 * 16)
            pool.wait_ge(idx_made, 1)
            for j in range(SJ):
                fetch(0, 0, j)

            def put(e, k, j):
                pool.wait_ge(done_made, e * SJ + j + 1 + SJ)
                apart(pool)
                g_.indirect_dma_start(
                    out[:, :], bass.IndirectOffsetOnAxis(ap=put_idx[k][:, j:j + 1], axis=0),
                    back[j][:, 0:D], None, bounds_check=T - 1, oob_is_err=False).then_inc(out_put[j], 16)

            def expert(e, k, far):
                if far:
                    top(e + 2)
                for j in range(SJ):
                    pool.wait_ge(gate_made, e * SJ + j + 1 + 2 * SJ)
                    pool.wait_ge(back_in[j], e * 16 + 16)
                    g_.tensor_tensor(gate[:, j, :], gate[:, j, :], back[j][:, D:2 * D], ALU.mult).then_inc(gated, 1)
                    pool.wait_ge(gated, e * SJ + j + 1)
                    g_.tensor_tensor(back[j][:, 0:D], gate[:, j, :], back[j][:, 0:D], ALU.add).then_inc(done_made, 1)
                    put(e, k, j)
                for j in range(SJ):
                    pool.wait_ge(out_put[j], e * 16 + 16)
                pool.sem_inc(put_over, 1)
                pool.wait_ge(idx_made, e + 2)
                apart(pool)
                for j in range(SJ):
                    fetch(e + 1, 1 - k, j)

            with pool.Fori(0, E // 2 - 1) as i:
                for k in range(2):
                    expert(i * 2 + k, k, True)
            expert(E - 2, 0, False)
            for j in range(SJ):
                put(E - 1, 1, j)
            for j in range(SJ):
                pool.wait_ge(out_put[j], 16 * E)

        @block.vector
        def _(dve):
            v = nc.vector
            count = [0]

            def step(ins, at=0):
                count[0] += 1
                ins.then_inc(dve_step, 1)
                dve.wait_ge(dve_step, at + count[0])

            def norm_stats(g, tiles):
                k = g % 2
                dve.wait_ge(x_in[k], (g // 2 + 1) * 16)
                for j in tiles:
                    last = v.bn_stats(stats[:, j, :], xg[k][:, j, :])
                step(last)

            def norm_var(g):
                if g:
                    dve.wait_ge(xn_made, g)
                for j in range(GT):
                    last = v.bn_aggr(mv[:, j, :], stats[:, j, :])
                step(last)
                v.tensor_scalar(var[:, :], mv[:, :, 1], EPS, None, ALU.add).then_inc(var_made, 1)

            def normed(g):
                dve.wait_ge(rstd_made, g + 1)
                for j in range(GT):
                    last = v.tensor_scalar(xnr[g][:, j, 0:D], xg[g][:, j, :], mv[:, j, 0:1], rstd[:, j:j + 1],
                                           ALU.subtract, ALU.mult)
                last.then_inc(xn_made, 1)

            norm_stats(0, range(GT))
            norm_var(0)

            dve.wait_ge(small_in, 64)
            v.tensor_reduce(small_max[:, 0:1], wsmall[:, 0], AX.XY, ALU.max, apply_absolute_value=True)
            v.tensor_reduce(small_max[:, 1:2], wsmall[:, 1], AX.XY, ALU.max, apply_absolute_value=True)
            v.tensor_reduce(small_max[:, 2:3], wsmall[:, 2, :, 0:E], AX.XY, ALU.max, apply_absolute_value=True
                            ).then_inc(small_maxed, 1)

            def scales(top, exp, up, dn, at=0):
                step(v.tensor_scalar(exp, top, 2.0 ** -100, None, ALU.max), at)
                step(v.tensor_scalar(exp.bitcast(I32), exp.bitcast(I32), 0x7F800000, None, ALU.bitwise_and), at)
                step(v.tensor_scalar(up.bitcast(I32), exp.bitcast(I32), float((2 * 127 + W_TOP) << 23), -1.0,
                                     ALU.subtract, ALU.mult), at)
                step(v.tensor_scalar(dn.bitcast(I32), exp.bitcast(I32), float(W_TOP << 23), None, ALU.subtract), at)

            dve.wait_ge(consts_made, 8)
            normed(0)
            dve.wait_ge(small_topped, 1)
            scales(small_top[:, :], small_exp[:, :], small_up[:, :], small_dn[:, :])
            v.tensor_scalar(score_mul[:, :], small_dn[:, 0:1], SM_SCALE * UNDO / X_UP, None, ALU.mult)
            v.tensor_scalar(value_mul[:, :], small_dn[:, 1:2], UNDO, None, ALU.mult)
            v.tensor_scalar(logit_mul[:, :], small_dn[:, 2:3], 1.0 / X_UP, None, ALU.mult)
            v.tensor_scalar(bias_mul[:, :], small_up[:, 0:1], X_UP / (SM_SCALE * UNDO), None, ALU.mult
                            ).then_inc(small_scaled, 1)

            def query_weights():
                dve.wait_ge(small_hi, 1)
                v.scalar_tensor_tensor(wqk_l[:, :, :], wsmall[:, 0], small_up[:, 0:1], wqk_h[:, :, :],
                                       ALU.mult, ALU.subtract).then_inc(ready, 1)

            def value_weights():
                dve.wait_ge(small_hi, 2)
                v.scalar_tensor_tensor(wvr_l[:, :, D:D + E], wsmall[:, 2, :, 0:E], small_up[:, 2:3],
                                       wvr_h[:, :, D:D + E], ALU.mult, ALU.subtract)
                for k in range(KD):
                    dve.wait_ge(small_hi, 3 + k)
                    last = v.scalar_tensor_tensor(wvr_l[:, k, 0:D], tr_ps[k][:, 0:D], small_up[:, 1:2],
                                                  wvr_h[:, k, 0:D], ALU.mult, ALU.subtract)
                last.then_inc(values_ready, 1)

            def bias_table():
                dve.wait_ge(bias_raw, 1)
                v.tensor_scalar(bias[:, :], bias[:, :], slope_c[:, 0:1], bias_mul[:, 0:1], ALU.mult, ALU.mult
                                ).then_inc(bias_made, 1)

            def unit(g, n):
                u = g * UNITS + n
                a, at = aux[u % 2], key_slot(g // NG, g % NG)
                if n < HALVED:
                    dve.wait_ge(hi_made, g * HALVED + n + 1)
                if n < QRY:
                    v.scalar_tensor_tensor(xT_l[:, n, at, :], a[:, :], X_UP, xT_h[:, n, at, :],
                                           ALU.mult, ALU.subtract).then_inc(aux_read, 1)
                elif n < VAL:
                    v.scalar_tensor_tensor(qT_l[g % 2][:, n - QRY, :], a[:, :], ACC_DOWN, qT_h[g % 2][:, n - QRY, :],
                                           ALU.mult, ALU.subtract).then_inc(aux_read, 1)
                elif n < RANK:
                    j = n - VAL
                    v.scalar_tensor_tensor(v_l[:, at, j, :], a[:, 0:D], ACC_DOWN, v_h[:, at, j, :],
                                           ALU.mult, ALU.subtract)
                    v.tensor_scalar(logits[:, j, :], a[:, D:D + E], logit_mul[:, 0:1], None, ALU.mult
                                    ).then_inc(aux_read, 1)
                    if j == GT - 1:
                        choose(g, u)
                else:
                    dve.wait_ge(aux_full, u + 1)
                    v.tensor_copy(counts[:, :, :], a[:, 0:(GT + 1) * E].rearrange("p (j e) -> p j e", e=E)
                                  ).then_inc(aux_read, 1)

            def choose(g, u):
                dve.wait_ge(aux_read, u + 1)
                if g:
                    dve.wait_ge(slot_made, g)
                step(v.tensor_reduce(lmax[:, :], logits[:, :, :], AX.X, ALU.max))
                v.tensor_tensor(below[:, :, :], logits[:, :, :], lmax[:, :].unsqueeze(2).to_broadcast([P, GT, E]),
                                ALU.subtract).then_inc(below_made, 1)
                dve.wait_ge(below_made, g + 1)
                step(v.scalar_tensor_tensor(key[:, :, :], below[:, :, :], 0.0, ranks[:, :, :],
                                            ALU.is_equal, ALU.mult))
                step(v.tensor_reduce(kmax[:, :], key[:, :, :], AX.X, ALU.max))
                v.tensor_tensor(chosen[:, :, :], key[:, :, :], kmax[:, :].unsqueeze(2).to_broadcast([P, GT, E]),
                                ALU.is_equal).then_inc(chosen_made, 1)
                v.tensor_scalar(limit[:, :], kmax[:, :], -float(CAP), float((E + 1) * CAP), ALU.mult, ALU.add)
                dve.wait_ge(lexp_made, g + 1)
                step(v.tensor_reduce(lsum[:, :], lexp[:, :, :], AX.X, ALU.add))
                v.reciprocal(xnr[g % 2][:, :, PCOL], lsum[:, :]).then_inc(prob_set, 1)

            def score(t, c):
                n, w, k = chunk_no(t, c), chunk_blocks(t, c) * P, t % 2
                lo = S - P - t % NT * P + c * GTOK
                dve.wait_ge(score_full, n + 1)
                v.tensor_tensor_reduce(sc[:, k, c * GTOK:c * GTOK + w], sc_ps[n % 2][:, 0:w], bias[:, lo:lo + w],
                                       score_mul[:, 0:1], -3e38, ALU.add, ALU.max, cmax[:, k, c:c + 1]
                                       ).then_inc(score_read, 1)
                if c == chunks(t) - 1:
                    dve.wait_ge(score_read, n + 1)
                    step(v.tensor_reduce(rmax[:, k:k + 1], cmax[:, k, 0:c + 1], AX.X, ALU.max))
                    v.tensor_scalar(nbias[:, k:k + 1], rmax[:, k:k + 1], -1.0, LN2_UP, ALU.mult, ALU.add
                                    ).then_inc(nbias_made, 1)

            def low(t, c):
                n, w = chunk_no(t, c), chunk_blocks(t, c) * P
                cols = slice(c * GTOK, c * GTOK + w)
                dve.wait_ge(pT_hi, n + 1)
                v.tensor_tensor(pT_l[:, t % 2, cols], tr_ps[n % 2][:, 0:w], pT_h[:, t % 2, cols], ALU.subtract
                                ).then_inc(pT_lo, 1)

            def finish(t):
                k, g = t % 2, t // GT
                step(v.tensor_reduce(rsum[:, k:k + 1], psums[:, t % 3, 0:chunks(t)], AX.X, ALU.add))
                step(v.reciprocal(rinv[:, k:k + 1], rsum[:, k:k + 1]))
                dve.wait_ge(pv_full, t + 1)
                if t % GT == 0 and g >= 2:
                    dve.wait_ge(rows_s[g % 2], g // 2 * 16)
                v.tensor_scalar(so[g % 2][:, t % GT, :], pv_ps[k][:, 0:D], rinv[:, k:k + 1], value_mul[:, 0:1],
                                ALU.mult, ALU.mult).then_inc(s_made, 1)

            def largest(buf, q, at=0):
                m, cols = piece(q)
                last = v.tensor_reduce(pmax[:, m, q % PIECES:q % PIECES + 1], buf[:, m, cols], AX.X, ALU.max,
                                       apply_absolute_value=True)
                if q == 2 * PIECES - 1:
                    step(last, at)
                    v.tensor_reduce(wmax[:, :], pmax[:, :, :], AX.X, ALU.max).then_inc(w_maxed, 1)

            def scale(e, k, at=0):
                dve.wait_ge(w_topped, e + 1)
                scales(wtop[:, :], wexp[:, :], wup[k][:, :], wdn[:, :], at)
                v.tensor_scalar(ymul[k][:, :], wdn[:, 0:1], wdn[:, 1:2], UNDO, ALU.mult, ALU.mult
                                ).then_inc(w_scaled, 1)

            def split_low(buf, e, k, q):
                m, cols = piece(q)
                dve.wait_ge(w_hi, e * 2 * PIECES + q + 1)
                v.scalar_tensor_tensor(w_l[k][:, m, cols], buf[:, m, cols], wup[k][:, m:m + 1], w_h[k][:, m, cols],
                                       ALU.mult, ALU.subtract).then_inc(w_lo, 1)

            def take_rows(k):
                v.tensor_scalar(pk[k][:, :], xe[:, :, PCOL], ymul[k][:, 0:1], None, ALU.mult)
                v.tensor_scalar(get_idx[k][:, :], xe[:, :, TCOL], float(T - 1), None, ALU.min)
                v.tensor_copy(put_idx[k][:, :], xe[:, :, TCOL]).then_inc(idx_made, 1)

            def turn_low(e, k, d):
                dve.wait_ge(xe_hi, e * KD + d + 1)
                v.scalar_tensor_tensor(xeT_l[k][:, d, :], aux[d][:, :], X_UP, xeT_h[k][:, d, :],
                                       ALU.mult, ALU.subtract).then_inc(xe_lo, 1)

            def hidden(m, f):
                dve.wait_ge(h_hi, m + 1)
                v.tensor_tensor(hid_l[:, f % HB, :], hid[:, f % 2, :], hid_h[:, f % HB, :], ALU.subtract
                                ).then_inc(h_lo, 1)

            for n in range(RANK):
                unit(0, n)
                if n == XT + 1:
                    query_weights()
                    value_weights()
                    norm_stats(1, range(GT))
                    norm_var(1)
                if n == QRY + 1:
                    bias_table()
                if n == VAL:
                    dve.wait_ge(masked, 1)
                    score(0, 0)
                if n == VAL + 1:
                    normed(1)
            for t in range(TILES):
                for c in steps(t):
                    if c < chunks(t + 1):
                        score(t + 1, c)
                    if c < chunks(t):
                        low(t, c)
                    if c == chunks(t - 1) - 1:
                        finish(t - 1)
                    for g, n in units_after(t, c):
                        unit(g, n)
                if t % GT < 2 and t // GT + 2 < GROUPS and t // GT != NG:
                    norm_stats(t // GT + 2, range(t % GT * 2, t % GT * 2 + 2))
                    if t % GT:
                        norm_var(t // GT + 2)
                if t == NT - 1:
                    norm_stats(NG + 2, range(GT))
                    norm_var(NG + 2)
                for q in share(FIRST_MAX, t):
                    dve.wait_ge(w_in[1], 16)
                    largest(raw, q)
                if t == FIRST_SCALE:
                    scale(0, 0)
                for q in share(FIRST_SPLIT, t):
                    split_low(raw, 0, 0, q)
                for q in share(SECOND_MAX, t):
                    dve.wait_ge(w_in[1], 32)
                    largest(raw, q)
                if t == FIRST_ROWS:
                    for d in range(KD):
                        turn_low(0, 0, d)
                    dve.wait_ge(w_scaled, 1)
                    take_rows(0)
            hidden(0, 0)
            finish(TILES - 1)
            hidden(1, 1)
            first_steps = count[0]

            def expert(i, k, more, far, at):
                e, o = i * 2 + k, 1 - k
                for f in range(NF):
                    if more or f + LEAD < NF:
                        hidden(e * NF + f + LEAD, f + LEAD)
                    if more:
                        if f == 0:
                            scale(e + 1, o, at)
                        if f in TURN_AT:
                            turn_low(e + 1, o, TURN_AT.index(f))
                        for q in SPLIT_AT.get(f, ()):
                            split_low(wraw[o], e + 1, o, q)
                        if f == NF - 2:
                            dve.wait_ge(xe_in, e * 16 + 32)
                            dve.wait_ge(w_scaled, e + 2)
                            dve.wait_ge(put_over, e + 1)
                            take_rows(o)
                    if far:
                        if f == min(MAX_AT):
                            dve.wait_ge(w_in[k], i * 16 + (48 if k else 16))
                        for q in MAX_AT.get(f, ()):
                            largest(wraw[k], q, at)

            with dve.Fori(0, E // 2 - 1) as i:
                count[0] = 0
                for k in range(2):
                    expert(i, k, True, True, i * PAIR_STEPS + first_steps)
                assert count[0] == PAIR_STEPS, count[0]
            count[0] = 0
            expert(E // 2 - 1, 0, True, False, (E // 2 - 1) * PAIR_STEPS + first_steps)
            expert(E // 2 - 1, 1, False, False, 0)
            for j in range(SJ):
                dve.wait_ge(gate_made, (E - 1) * SJ + j + 1 + 2 * SJ)
                dve.wait_ge(back_in[j], E * 16)
                v.tensor_tensor(gate[:, j, :], gate[:, j, :], back[j][:, D:2 * D], ALU.mult).then_inc(gated, 1)
                dve.wait_ge(gated, (E - 1) * SJ + j + 1)
                v.tensor_tensor(back[j][:, 0:D], gate[:, j, :], back[j][:, 0:D], ALU.add).then_inc(done_made, 1)

        @block.scalar
        def _(act):
            a_ = nc.scalar
            act.dma_start(xg[0][:, :, :], x_g[0]).then_inc(x_in[0], 16)

            def unit(g, n):
                if n == RANK:
                    return
                u = g * UNITS + n
                a, at = aux[u % 2], key_slot(g // NG, g % NG)
                act.wait_ge(aux_full, u + 1)
                if n < QRY:
                    a_.activation(xT_h[:, n, at, :], a[:, :], ACT.Copy, scale=X_UP).then_inc(hi_made, 1)
                elif n < VAL:
                    a_.activation(qT_h[g % 2][:, n - QRY, :], a[:, :], ACT.Copy, scale=ACC_DOWN).then_inc(hi_made, 1)
                else:
                    a_.activation(v_h[:, at, n - VAL, :], a[:, 0:D], ACT.Copy, scale=ACC_DOWN).then_inc(hi_made, 1)
                    if n == RANK - 1:
                        act.wait_ge(below_made, g + 1)
                        a_.activation(lexp[:, :, :], below[:, :, :], ACT.Exp).then_inc(lexp_made, 1)

            def probs(t, cs):
                k = t % 2
                act.wait_ge(nbias_made, t + 1)
                for c in cs:
                    cols = slice(c * GTOK, c * GTOK + chunk_blocks(t, c) * P)
                    a_.activation(sc[:, k, cols], sc[:, k, cols], ACT.Exp, bias=nbias[:, k:k + 1],
                                  accum_out=psums[:, t % 3, c:c + 1]).then_inc(exp_made, 1)

            def high(t, c):
                n, w = chunk_no(t, c), chunk_blocks(t, c) * P
                act.wait_ge(turned, n + 1)
                a_.activation(pT_h[:, t % 2, c * GTOK:c * GTOK + w], tr_ps[n % 2][:, 0:w], ACT.Copy
                              ).then_inc(pT_hi, 1)

            def split_high(buf, e, k, q):
                m, cols = piece(q)
                act.wait_ge(w_scaled, e + 1)
                a_.activation(w_h[k][:, m, cols], buf[:, m, cols], ACT.Copy, scale=wup[k][:, m:m + 1]
                              ).then_inc(w_hi, 1)

            def turn_high(e, k, d):
                act.wait_ge(xe_turned, e * KD + d + 1)
                a_.activation(xeT_h[k][:, d, :], aux[d][:, :], ACT.Copy, scale=X_UP).then_inc(xe_hi, 1)

            def hidden(m, f, first=False):
                act.wait_ge(h_full, m + 1)
                if not first:
                    act.wait_ge(h_lo, m - 1)
                a_.activation(hid[:, f % 2, :], sc_ps[f % 2][:, :], ACT.Relu, scale=ACC_DOWN).then_inc(h_read, 1)
                act.wait_ge(h_read, m + 1)
                a_.activation(hid_h[:, f % HB, :], hid[:, f % 2, :], ACT.Copy).then_inc(h_hi, 1)

            def small_highs():
                act.wait_ge(small_scaled, 1)
                a_.activation(wqk_h[:, :, :], wsmall[:, 0], ACT.Copy, scale=small_up[:, 0:1]).then_inc(small_hi, 1)
                a_.activation(wvr_h[:, :, D:D + E], wsmall[:, 2, :, 0:E], ACT.Copy, scale=small_up[:, 2:3]
                              ).then_inc(small_hi, 1)
                for k in range(KD):
                    act.wait_ge(wv_turned, k + 1)
                    a_.activation(wvr_h[:, k, 0:D], tr_ps[k][:, 0:D], ACT.Copy, scale=small_up[:, 1:2]
                                  ).then_inc(small_hi, 1)

            for n in range(RANK):
                unit(0, n)
                if n == XT + 1:
                    small_highs()
                if n == VAL:
                    probs(0, range(1))
            for t in range(TILES):
                for c in steps(t):
                    if c < chunks(t):
                        high(t, c)
                    ahead = min(chunks(t + 1), 2) if last_step(t, c) and (c or t % GT != 1) else 0
                    if ahead:
                        probs(t + 1, range(ahead))
                    for g, n in units_after(t, c):
                        unit(g, n)
                if ahead < chunks(t + 1):
                    probs(t + 1, range(ahead, chunks(t + 1)))
                for q in share(FIRST_SPLIT, t):
                    split_high(raw, 0, 0, q)
                if t == FIRST_ROWS:
                    for d in range(KD):
                        turn_high(0, 0, d)
            act.wait_ge(consts_made, 1)
            a_.activation(warm[:, :], empty[:, 0:1], ACT.Silu)
            for f in range(LEAD):
                hidden(f, f, True)

            def expert(i, k, more):
                e, o = i * 2 + k, 1 - k
                for f in range(NF):
                    if more or f + LEAD < NF:
                        hidden(e * NF + f + LEAD, f + LEAD)
                    if more:
                        if f in TURN_AT:
                            turn_high(e + 1, o, TURN_AT.index(f))
                        for q in SPLIT_AT.get(f, ()):
                            split_high(wraw[o], e + 1, o, q)
                act.wait_ge(idx_made, e + 1)
                for j in range(SJ):
                    act.wait_ge(y_full, e * (SJ // 2) + j // 2 + 1)
                    act.wait_ge(done_made, e * SJ + SJ)
                    a_.activation(gate[:, j, :], y_ps[k][j], ACT.Silu, scale=pk[k][:, j:j + 1]).then_inc(gate_made, 1)

            with act.Fori(0, E // 2 - 1) as i:
                for k in range(2):
                    expert(i, k, True)
            expert(E // 2 - 1, 0, True)
            expert(E // 2 - 1, 1, False)

        @block.tensor
        def _(pe):
            def product(ps, a_h, a_l, b_h, b_l, first, last, shared=False):
                pe.matmul(ps, a_h, b_h, start=first, stop=False, skip_group_check=shared)
                pe.matmul(ps, a_h, b_l, start=False, stop=False, skip_group_check=shared)
                return pe.matmul(ps, a_l, b_h, start=False, stop=last, skip_group_check=shared)

            def unit(g, n):
                u = g * UNITS + n
                a, at = aux[u % 2], key_slot(g // NG, g % NG)
                if u >= 2:
                    pe.wait_ge(aux_read, u - 1)
                if n < QRY:
                    if n == 0:
                        pe.wait_ge(xn_made, g + 1)
                    for j in range(GT):
                        last = pe.transpose(a[:, j * P:(j + 1) * P], xnr[g % 2][:, j, n * P:(n + 1) * P], ident[:, :])
                elif n < VAL:
                    if n == QRY:
                        pe.wait_ge(aux_read, u)
                        if g == 0:
                            pe.wait_ge(ready, 1)
                    cols = slice((n - QRY) * P, (n - QRY + 1) * P)
                    for d in range(KD):
                        last = product(a[:, :], wqk_h[:, d, cols], wqk_l[:, d, cols],
                                       xT_h[:, d, at, :], xT_l[:, d, at, :], d == 0, d == KD - 1)
                elif n < RANK:
                    if u == VAL:
                        pe.wait_ge(values_ready, 1)
                    rows_ = slice((n - VAL) * P, (n - VAL + 1) * P)
                    for d in range(KD):
                        last = product(a[:, 0:D + E], xT_h[:, d, at, rows_], xT_l[:, d, at, rows_],
                                       wvr_h[:, d, :], wvr_l[:, d, :], d == 0, d == KD - 1)
                else:
                    pe.wait_ge(chosen_made, g + 1)
                    pe.matmul(a[:, 0:GT * E], before[:, :], chosen[:, :, :], start=True, stop=False,
                              skip_group_check=True)
                    for j in range(GT - 1):
                        pe.matmul(a[:, (j + 1) * E:GT * E], ones[:, :],
                                  chosen[:, j:j + 1, :].to_broadcast([P, GT - 1 - j, E]),
                                  start=False, stop=False, skip_group_check=True)
                    for j in range(GT):
                        last = pe.matmul(a[:, GT * E:GT * E + E], ones[:, :], chosen[:, j, :], start=False,
                                         stop=j == GT - 1, skip_group_check=True)
                last.then_inc(aux_full, 1)

            def score(t, c):
                n, w, g = chunk_no(t, c), chunk_blocks(t, c) * P, t // GT
                at = key_slot(t // NT, c)
                if c == 0 and t % GT == 0:
                    pe.wait_ge(aux_read, g * UNITS + VAL)
                if n >= 2:
                    pe.wait_ge(score_read, n - 1)
                rows_ = slice(t % GT * P, (t % GT + 1) * P)
                for d in range(KD):
                    last = product(sc_ps[n % 2][:, 0:w], qT_h[g % 2][:, d, rows_], qT_l[g % 2][:, d, rows_],
                                   xT_h[:, d, at, 0:w], xT_l[:, d, at, 0:w], d == 0, d == KD - 1)
                last.then_inc(score_full, 1)

            def turn(t, c):
                n = chunk_no(t, c)
                pe.wait_ge(exp_made, n + 1)
                if n >= 2:
                    pe.wait_ge(pT_lo, n - 1)
                for q in range(chunk_blocks(t, c)):
                    col = c * GTOK + q * P
                    last = pe.transpose(tr_ps[n % 2][:, q * P:(q + 1) * P], sc[:, t % 2, col:col + P], ident[:, :])
                last.then_inc(turned, 1)

            def values(t, c):
                n, at = chunk_no(t, c), key_slot(t // NT, c)
                pe.wait_ge(pT_lo, n + 1)
                if c == chunks(t) - 1:
                    pe.wait_ge(aux_read, t // GT * UNITS + VAL + t % GT + 1)
                if c == 0 and t >= 2:
                    pe.wait_ge(s_made, t - 1)
                for q in range(chunk_blocks(t, c)):
                    kb = c * GT + q
                    rows_ = slice(kb * P, (kb + 1) * P)
                    last = product(pv_ps[t % 2][:, 0:D], pT_h[:, t % 2, rows_], pT_l[:, t % 2, rows_],
                                   v_h[:, at, q, :], v_l[:, at, q, :], kb == 0, kb == t % NT)
                if c == chunks(t) - 1:
                    last.then_inc(pv_full, 1)

            def turn_rows(e, d):
                if d == 0:
                    pe.wait_ge(xe_in, e * 16 + 16)
                for j in range(SJ):
                    last = pe.transpose(aux[d][:, j * P:(j + 1) * P], xe[:, j, d * P:(d + 1) * P], ident[:, :])
                last.then_inc(xe_turned, 1)

            def up(e, f, k, first=False):
                if f == 0:
                    pe.wait_ge(w_lo, e * 2 * PIECES + PIECES)
                    pe.wait_ge(xe_lo, e * KD + KD)
                if not first:
                    pe.wait_ge(h_read, e * NF + f - 1)
                for d in range(KD):
                    cols = slice(d * F + f * P, d * F + (f + 1) * P)
                    last = product(sc_ps[f % 2][:, :], w_h[k][:, 0, cols], w_l[k][:, 0, cols],
                                   xeT_h[k][:, d, :], xeT_l[k][:, d, :], d == 0, d == KD - 1)
                last.then_inc(h_full, 1)

            def down(e, f, k, tiles=range(SJ)):
                if f == 0:
                    pe.wait_ge(w_lo, (e + 1) * 2 * PIECES)
                    pe.wait_ge(gate_made, (e + 1) * SJ)
                pe.wait_ge(h_lo, e * NF + f + 1)
                cols = slice(f * D, (f + 1) * D)
                for j in tiles:
                    rows_ = slice(j * P, (j + 1) * P)
                    last = product(y_ps[k][j], hid_h[:, f % HB, rows_], hid_l[:, f % HB, rows_],
                                   w_h[k][:, 1, cols], w_l[k][:, 1, cols], f == 0 and j % 2 == 0, f == NF - 1, True)
                    if f == NF - 1 and j % 2:
                        last.then_inc(y_full, 1)

            pe.wait_ge(small_in, 64)
            pe.wait_ge(consts_made, 8)
            for k in range(KD):
                for j in range(KD):
                    last = pe.transpose(tr_ps[k][:, j * P:(j + 1) * P], wsmall[:, 1, j, k * P:(k + 1) * P], ident[:, :])
                last.then_inc(wv_turned, 1)
            def warm_up(n):
                for _ in range(n):
                    pe.matmul(pv_ps[0][:, :], ones[:, :], before[:, :].unsqueeze(1).to_broadcast([P, 4, P]),
                              start=True, stop=True)

            warm_up(9)
            for n in range(RANK):
                if n == QRY:
                    warm_up(9)
                unit(0, n)
                if n == QRY + 1:
                    score(0, 0)
            for t in range(TILES):
                for c in steps(t):
                    if c < chunks(t + 1):
                        score(t + 1, c)
                    if c < chunks(t - 1):
                        values(t - 1, c)
                    if c < chunks(t):
                        turn(t, c)
                    for g, n in units_after(t, c):
                        unit(g, n)
                if t == FIRST_ROWS:
                    pe.wait_ge(aux_read, GROUPS * UNITS)
                    for d in range(KD):
                        turn_rows(0, d)
            pe.wait_ge(score_read, ALL_CHUNKS)
            up(0, 0, 0, True)
            for c in range(chunks(TILES - 1)):
                values(TILES - 1, c)
            up(0, 1, 0, True)
            pe.wait_ge(s_made, TILES)

            def expert(i, k, more):
                e, o = i * 2 + k, 1 - k
                for f in range(NF):
                    if f + LEAD < NF:
                        up(e, f + LEAD, k)
                    elif more:
                        up(e + 1, f + LEAD - NF, o)
                    if more and f in TURN_AT:
                        d = TURN_AT.index(f)
                        pe.wait_ge(xe_lo, e * KD + d + 1)
                        turn_rows(e + 1, d)
                    if more or f < NF - LEAD:
                        down(e, f, k)
                if not more:
                    for j in range(0, SJ, 2):
                        for f in range(NF - LEAD, NF):
                            down(e, f, k, range(j, j + 2))

            with pe.Fori(0, E // 2 - 1) as i:
                for k in range(2):
                    expert(i, k, True)
            expert(E // 2 - 1, 0, True)
            expert(E // 2 - 1, 1, False)



def kernel(**inputs):
    import numpy as np
    import concourse.bacc as bacc
    from concourse.bass_utils import run_bass_kernel_spmd

    def plain(name):
        return np.ascontiguousarray(np.asarray(inputs[name]))

    w1 = plain("L0_ffn_W1").reshape(E, KD, P, F).transpose(0, 2, 1, 3).reshape(E, P, WCOLS)
    w2 = plain("L0_ffn_W2").reshape(E, NF, P, D).transpose(0, 2, 1, 3).reshape(E, P, WCOLS)
    arrays = {
        "in_x": plain("L0_attn_x").reshape(T, D), "in_w_qk": plain("L0_attn_W_qk"), "in_w_v": plain("L0_attn_W_v"),
        "in_slope": plain("L0_attn_alibi_slope"), "in_w_r": plain("L0_ffn_Wr"),
        "in_w_e": np.ascontiguousarray(np.stack([w1, w2], axis=1)),
    }
    nc = bacc.Bacc("TRN2", target_bir_lowering=False, num_devices=1)
    args = [nc.dram_tensor(n, a.shape, mybir.dt.from_np(a.dtype), kind="ExternalInput").ap()
            for n, a in arrays.items()]
    args.append(nc.dram_tensor("out_0", (T, D), F32, kind="ExternalOutput").ap())
    args.append(nc.dram_tensor("slots", (T, ROW), F32).ap())
    args.append(nc.dram_tensor("rows", (T, 2 * D), F32).ap())
    layer_kernel(nc, *args)
    r = run_bass_kernel_spmd(nc, [arrays], core_ids=[0])
    return r.results[0]["out_0"].reshape(B, S, D)
```
